# Optimizing a Trainium2 kernel written in Bass

```python
import numpy as np
import jax
import jax.numpy as jnp

def _softmax(x, axis=-1):
    return jax.nn.softmax(x, axis=axis)

def _gelu(x):
    return jax.nn.gelu(x, approximate=True)

def _silu(x):
    return jax.nn.silu(x)

def _sigmoid(x):
    return jax.nn.sigmoid(x)

def _layernorm(x, axis=-1, eps=1e-05):
    m = jnp.mean(x, axis=axis, keepdims=True)
    v = jnp.var(x, axis=axis, keepdims=True)
    return (x - m) / jnp.sqrt(v + eps)

def _scatter_add(tgt, idx, src, axis=0):
    return tgt.at[idx].add(src)

def _segment_sum(src, seg, n):
    return jax.ops.segment_sum(src, seg, n)
kernel_name = 'mk_seq_postln_d2_jaxref_r8_fefa76'

def setup_inputs(seed: int=0):
    np.random.seed(seed)
    _w = jnp.asarray

    def _L0_attn_setup():
        import jax, jax.numpy as jnp
        import numpy as np
        import math
        DIM = 512
        N_HEADS = 32
        N_KV_HEADS = 8
        HEAD_DIM = DIM // N_HEADS
        N_REP = N_HEADS // N_KV_HEADS
        ROPE_BASE = 10000.0

        def apply_rotary_emb(x):
            b, s, h, d = x.shape
            inv_freq = 1.0 / ROPE_BASE ** (jnp.arange(0, d, 2, dtype=jnp.float32) / d)
            pos = jnp.arange(s, dtype=jnp.float32)
            ang = pos[:, None] * inv_freq[None, :]
            cos = jnp.cos(ang)[None, :, None, :]
            sin = jnp.sin(ang)[None, :, None, :]
            xr = x.reshape(b, s, h, d // 2, 2)
            x0, x1 = (xr[..., 0], xr[..., 1])
            out = jnp.stack([x0 * cos - x1 * sin, x0 * sin + x1 * cos], axis=-1)
            return out.reshape(b, s, h, d)
        key = jax.random.key(seed)
        ks = jax.random.split(key, 5)
        sc = 1.0 / math.sqrt(DIM)
        return {'x': jax.random.normal(ks[0], (2, 256, DIM), dtype=jnp.float32), 'Wq': jax.random.normal(ks[1], (DIM, N_HEADS * HEAD_DIM), dtype=jnp.float32) * sc, 'Wk': jax.random.normal(ks[2], (DIM, N_KV_HEADS * HEAD_DIM), dtype=jnp.float32) * sc, 'Wv': jax.random.normal(ks[3], (DIM, N_KV_HEADS * HEAD_DIM), dtype=jnp.float32) * sc, 'Wo': jax.random.normal(ks[4], (N_HEADS * HEAD_DIM, DIM), dtype=jnp.float32) * sc}
    _L0_attn_in = _L0_attn_setup()

    def _L0_ffn_setup():
        import jax, jax.numpy as jnp
        import numpy as np

        def sparsemax(z):
            E = z.shape[-1]
            z_sorted = -jnp.sort(-z, axis=-1)
            z_cum = jnp.cumsum(z_sorted, axis=-1)
            k = jnp.arange(1, E + 1, dtype=z.dtype)
            support = 1.0 + k * z_sorted > z_cum
            k_z = jnp.sum(support, axis=-1, keepdims=True)
            tau_sum = jnp.take_along_axis(z_cum, k_z.astype(jnp.int32) - 1, axis=-1)
            tau = (tau_sum - 1.0) / k_z.astype(z.dtype)
            return jnp.maximum(z - tau, 0.0)
        key = jax.random.key(seed)
        ks = jax.random.split(key, 6)
        B, S, D_IN, D_OUT, E, R = (8, 256, 512, 512, 8, 16)
        x = jax.random.normal(ks[0], (B, S, D_IN), dtype=jnp.float32)
        W_base = jax.random.normal(ks[1], (D_OUT, D_IN), dtype=jnp.float32) * D_IN ** (-0.5)
        b_base = jax.random.normal(ks[2], (D_OUT,), dtype=jnp.float32) * 0.01
        W_router = jax.random.normal(ks[3], (E, D_IN), dtype=jnp.float32) * D_IN ** (-0.5)
        b_router = jnp.zeros((E,), dtype=jnp.float32)
        lora_A = jax.random.normal(ks[4], (E, D_IN, R), dtype=jnp.float32) * D_IN ** (-0.5)
        lora_B = jnp.zeros((E, R, D_OUT), dtype=jnp.float32)
        return {'x': x, 'W_base': W_base, 'b_base': b_base, 'W_router': W_router, 'b_router': b_router, 'lora_A': lora_A, 'lora_B': lora_B}
    _L0_ffn_in = _L0_ffn_setup()

    def _L1_attn_setup():
        import jax, jax.numpy as jnp
        import numpy as np
        H, KV, HD, HID = (32, 8, 128, 512)
        THETA, FACTOR, HI_FF, LO_FF, ORIG_MAX = (500000.0, 8.0, 4.0, 1.0, 1024)

        def _llama3_inv_freq():
            inv = 1.0 / THETA ** (np.arange(0, HD, 2, dtype=np.float64) / HD)
            wavelen = 2.0 * np.pi / inv
            low_wl = ORIG_MAX / LO_FF
            high_wl = ORIG_MAX / HI_FF
            smooth = (ORIG_MAX / wavelen - LO_FF) / (HI_FF - LO_FF)
            scaled = np.where(wavelen > low_wl, inv / FACTOR, inv)
            mid = (wavelen <= low_wl) & (wavelen >= high_wl)
            scaled = np.where(mid, (1 - smooth) * inv / FACTOR + smooth * inv, scaled)
            return scaled.astype(np.float32)

        def _rope_cos_sin(T):
            inv = _llama3_inv_freq()
            pos = np.arange(T, dtype=np.float32)
            freqs = pos[:, None] * inv[None, :]
            emb = np.concatenate([freqs, freqs], axis=-1)
            return (jnp.asarray(np.cos(emb)), jnp.asarray(np.sin(emb)))

        def _rotate_half(x):
            x1, x2 = jnp.split(x, 2, axis=-1)
            return jnp.concatenate([-x2, x1], axis=-1)
        key = jax.random.key(seed)
        ks = jax.random.split(key, 5)
        s = 1.0 / np.sqrt(HID)
        return {'x': jax.random.normal(ks[0], (1, 256, HID), jnp.float32), 'wq': jax.random.normal(ks[1], (HID, H * HD), jnp.float32) * s, 'wk': jax.random.normal(ks[2], (HID, KV * HD), jnp.float32) * s, 'wv': jax.random.normal(ks[3], (HID, KV * HD), jnp.float32) * s, 'wo': jax.random.normal(ks[4], (H * HD, HID), jnp.float32) * s}
    _L1_attn_in = _L1_attn_setup()

    def _L1_ffn_setup():
        import jax, jax.numpy as jnp
        import numpy as np
        HIDDEN_SIZE = 512
        D_FF = 4 * HIDDEN_SIZE
        BATCH, SEQ = (2, 256)
        key = jax.random.key(seed)
        k0, k1, k2, k3, k4 = jax.random.split(key, 5)
        scale = 0.02
        return {'hidden_states': jax.random.normal(k0, (BATCH, SEQ, HIDDEN_SIZE), dtype=jnp.float32), 'W1': jax.random.normal(k1, (HIDDEN_SIZE, D_FF), dtype=jnp.float32) * scale, 'fc1_bias': jax.random.normal(k2, (D_FF,), dtype=jnp.float32) * scale, 'W2': jax.random.normal(k3, (D_FF, HIDDEN_SIZE), dtype=jnp.float32) * scale, 'fc2_bias': jax.random.normal(k4, (HIDDEN_SIZE,), dtype=jnp.float32) * scale}
    _L1_ffn_in = _L1_ffn_setup()
    _d = {'L0_attn_x': _L0_attn_in['x'], 'L0_attn_Wq': _L0_attn_in['Wq'], 'L0_attn_Wk': _L0_attn_in['Wk'], 'L0_attn_Wv': _L0_attn_in['Wv'], 'L0_attn_Wo': _L0_attn_in['Wo'], 'L0_ffn_W_base': _L0_ffn_in['W_base'], 'L0_ffn_b_base': _L0_ffn_in['b_base'], 'L0_ffn_W_router': _L0_ffn_in['W_router'], 'L0_ffn_b_router': _L0_ffn_in['b_router'], 'L0_ffn_lora_A': _L0_ffn_in['lora_A'], 'L0_ffn_lora_B': _L0_ffn_in['lora_B'], 'L1_attn_wq': _L1_attn_in['wq'], 'L1_attn_wk': _L1_attn_in['wk'], 'L1_attn_wv': _L1_attn_in['wv'], 'L1_attn_wo': _L1_attn_in['wo'], 'L1_ffn_W1': _L1_ffn_in['W1'], 'L1_ffn_fc1_bias': _L1_ffn_in['fc1_bias'], 'L1_ffn_W2': _L1_ffn_in['W2'], 'L1_ffn_fc2_bias': _L1_ffn_in['fc2_bias']}
    _x0 = _d['L0_attn_x']
    _d['L0_attn_x'] = jax.random.normal(jax.random.fold_in(jax.random.key(seed), 1), (8, 256, 512), dtype=_x0.dtype)
    del _x0
    return _d

def reference(L0_attn_x, L0_attn_Wq, L0_attn_Wk, L0_attn_Wv, L0_attn_Wo, L0_ffn_W_base, L0_ffn_b_base, L0_ffn_W_router, L0_ffn_b_router, L0_ffn_lora_A, L0_ffn_lora_B, L1_attn_wq, L1_attn_wk, L1_attn_wv, L1_attn_wo, L1_ffn_W1, L1_ffn_fc1_bias, L1_ffn_W2, L1_ffn_fc2_bias):

    def _L0_attn_ref(x, Wq, Wk, Wv, Wo):
        import jax, jax.numpy as jnp
        import numpy as np
        import math
        DIM = 512
        N_HEADS = 32
        N_KV_HEADS = 8
        HEAD_DIM = DIM // N_HEADS
        N_REP = N_HEADS // N_KV_HEADS
        ROPE_BASE = 10000.0

        def apply_rotary_emb(x):
            b, s, h, d = x.shape
            inv_freq = 1.0 / ROPE_BASE ** (jnp.arange(0, d, 2, dtype=jnp.float32) / d)
            pos = jnp.arange(s, dtype=jnp.float32)
            ang = pos[:, None] * inv_freq[None, :]
            cos = jnp.cos(ang)[None, :, None, :]
            sin = jnp.sin(ang)[None, :, None, :]
            xr = x.reshape(b, s, h, d // 2, 2)
            x0, x1 = (xr[..., 0], xr[..., 1])
            out = jnp.stack([x0 * cos - x1 * sin, x0 * sin + x1 * cos], axis=-1)
            return out.reshape(b, s, h, d)
        b, s, _ = x.shape
        xq = (x @ Wq).reshape(b, s, N_HEADS, HEAD_DIM)
        xk = (x @ Wk).reshape(b, s, N_KV_HEADS, HEAD_DIM)
        xv = (x @ Wv).reshape(b, s, N_KV_HEADS, HEAD_DIM)
        xq = apply_rotary_emb(xq)
        xk = apply_rotary_emb(xk)
        xk = jnp.repeat(xk, N_REP, axis=2)
        xv = jnp.repeat(xv, N_REP, axis=2)
        scores = jnp.einsum('bqhd,bkhd->bhqk', xq, xk) / math.sqrt(HEAD_DIM)
        causal = jnp.tril(jnp.ones((s, s), dtype=bool))
        scores = jnp.where(causal[None, None], scores, -jnp.inf)
        probs = jax.nn.softmax(scores.astype(jnp.float32), axis=-1).astype(xq.dtype)
        out = jnp.einsum('bhqk,bkhd->bqhd', probs, xv).reshape(b, s, N_HEADS * HEAD_DIM)
        return out @ Wo

    def _L0_ffn_ref(x, W_base, b_base, W_router, b_router, lora_A, lora_B):
        import jax, jax.numpy as jnp
        import numpy as np

        def sparsemax(z):
            E = z.shape[-1]
            z_sorted = -jnp.sort(-z, axis=-1)
            z_cum = jnp.cumsum(z_sorted, axis=-1)
            k = jnp.arange(1, E + 1, dtype=z.dtype)
            support = 1.0 + k * z_sorted > z_cum
            k_z = jnp.sum(support, axis=-1, keepdims=True)
            tau_sum = jnp.take_along_axis(z_cum, k_z.astype(jnp.int32) - 1, axis=-1)
            tau = (tau_sum - 1.0) / k_z.astype(z.dtype)
            return jnp.maximum(z - tau, 0.0)
        base_out = jnp.einsum('bsd,od->bso', x, W_base) + b_base
        logits = jnp.einsum('bsd,ed->bse', x, W_router) + b_router
        weights = sparsemax(logits)
        h = jnp.einsum('bsd,edr->bser', x, lora_A)
        expert_out = jnp.einsum('bser,bse,ero->bso', h, weights, lora_B)
        return base_out + expert_out

    def _L1_attn_ref(x, wq, wk, wv, wo):
        import jax, jax.numpy as jnp
        import numpy as np
        H, KV, HD, HID = (32, 8, 128, 512)
        THETA, FACTOR, HI_FF, LO_FF, ORIG_MAX = (500000.0, 8.0, 4.0, 1.0, 1024)

        def _llama3_inv_freq():
            inv = 1.0 / THETA ** (np.arange(0, HD, 2, dtype=np.float64) / HD)
            wavelen = 2.0 * np.pi / inv
            low_wl = ORIG_MAX / LO_FF
            high_wl = ORIG_MAX / HI_FF
            smooth = (ORIG_MAX / wavelen - LO_FF) / (HI_FF - LO_FF)
            scaled = np.where(wavelen > low_wl, inv / FACTOR, inv)
            mid = (wavelen <= low_wl) & (wavelen >= high_wl)
            scaled = np.where(mid, (1 - smooth) * inv / FACTOR + smooth * inv, scaled)
            return scaled.astype(np.float32)

        def _rope_cos_sin(T):
            inv = _llama3_inv_freq()
            pos = np.arange(T, dtype=np.float32)
            freqs = pos[:, None] * inv[None, :]
            emb = np.concatenate([freqs, freqs], axis=-1)
            return (jnp.asarray(np.cos(emb)), jnp.asarray(np.sin(emb)))

        def _rotate_half(x):
            x1, x2 = jnp.split(x, 2, axis=-1)
            return jnp.concatenate([-x2, x1], axis=-1)
        B, T, _ = x.shape
        q = (x @ wq).reshape(B, T, H, HD).transpose(0, 2, 1, 3)
        k = (x @ wk).reshape(B, T, KV, HD).transpose(0, 2, 1, 3)
        v = (x @ wv).reshape(B, T, KV, HD).transpose(0, 2, 1, 3)
        cos, sin = _rope_cos_sin(T)
        q = q * cos + _rotate_half(q) * sin
        k = k * cos + _rotate_half(k) * sin
        rep = H // KV
        k = jnp.repeat(k, rep, axis=1)
        v = jnp.repeat(v, rep, axis=1)
        scores = jnp.einsum('bhtd,bhsd->bhts', q, k) * (1.0 / np.sqrt(HD))
        mask = jnp.tril(jnp.ones((T, T), dtype=bool))
        scores = jnp.where(mask, scores, -jnp.inf)
        att = jax.nn.softmax(scores, axis=-1)
        out = jnp.einsum('bhts,bhsd->bhtd', att, v)
        out = out.transpose(0, 2, 1, 3).reshape(B, T, H * HD)
        return out @ wo

    def _L1_ffn_ref(hidden_states, W1, fc1_bias, W2, fc2_bias):
        import jax, jax.numpy as jnp
        import numpy as np
        HIDDEN_SIZE = 512
        D_FF = 4 * HIDDEN_SIZE
        BATCH, SEQ = (2, 256)
        orig_shape = hidden_states.shape
        x = hidden_states.astype(jnp.float32).reshape(-1, HIDDEN_SIZE)
        h = jax.nn.gelu(x @ W1 + fc1_bias)
        out = (h @ W2).reshape(orig_shape).astype(hidden_states.dtype)
        return out + fc2_bias
    x = L0_attn_x
    x = _layernorm(x + _L0_attn_ref(x, L0_attn_Wq, L0_attn_Wk, L0_attn_Wv, L0_attn_Wo), axis=-1)
    x = _layernorm(x + _L0_ffn_ref(x, L0_ffn_W_base, L0_ffn_b_base, L0_ffn_W_router, L0_ffn_b_router, L0_ffn_lora_A, L0_ffn_lora_B), axis=-1)
    x = _layernorm(x + _L1_attn_ref(x, L1_attn_wq, L1_attn_wk, L1_attn_wv, L1_attn_wo), axis=-1)
    x = _layernorm(x + _L1_ffn_ref(x, L1_ffn_W1, L1_ffn_fc1_bias, L1_ffn_W2, L1_ffn_fc2_bias), axis=-1)
    return x

_drawn_inputs = setup_inputs


def setup_inputs(seed=0):
    import zlib

    import numpy as np

    out = dict(_drawn_inputs(seed))
    spreads = {'L0_ffn_b_router': (0.0, 0.473), 'L0_ffn_lora_B': (0.0, 0.1)}
    factors = {'L0_ffn_b_base': 3.331, 'L1_ffn_fc1_bias': 5.447, 'L1_ffn_fc2_bias': 2.969}
    for name, (base, spread) in spreads.items():
        noise = np.random.default_rng([zlib.crc32(name.encode()), seed]).standard_normal(out[name].shape)
        drawn = base * np.exp(spread * noise) if base else spread * noise
        out[name] = jnp.asarray(drawn.astype(out[name].dtype))
    for name, factor in factors.items():
        out[name] = (out[name] * factor).astype(out[name].dtype)
    return out
```

```python
import numpy as np
import concourse.bass as bass
from concourse import mybir
from contextlib import ExitStack

F32 = mybir.dt.float32
F32R = mybir.dt.float32r
ALU = mybir.AluOpType
ACT = mybir.ActivationFunctionType
AX = mybir.AxisListType

P = 128
D = 512
KT = D // P
B, S = 8, 256
TT = S // P
NT = B * TT
BIG = 3.0e38
EPS = 1e-5


def product(pe, out, w, x, first=True, last=True):
    pe.matmul(out, w[0], x[0], start=first, stop=False)
    pe.matmul(out, w[0], x[1], start=False, stop=False)
    return pe.matmul(out, w[1], x[0], start=False, stop=last)


def halves(pair, *index):
    return tuple(t[index] for t in pair)


def layer0(nc, xT_in, x_in_t, w_qkv, w_o, w_base, w_lr, w_lb, b_base_row, b_router_row, cos_t, sin_t, mask_t, ident_t,
           inv_k, x2, x2T_hi, x2T_lo):
    H, G, HD, E, R = 32, 8, 16, 8, 16
    HP, NP = HD // 2, H // 2
    QW, KW = H * HD, G * HD
    SCALE = 0.25
    VC = 32
    with ExitStack() as ctx:
        def sb(name, shape, dt=F32):
            return ctx.enter_context(nc.sbuf_tensor("l0_" + name, shape, dt))

        def sem(name):
            return ctx.enter_context(nc.semaphore("l0_" + name))

        def pair(name, shape):
            return sb(name + "_hi", shape, F32R), sb(name + "_lo", shape, F32R)

        stage = sb("stage", [P, KT * (QW + 2 * KW)], F32R)
        raw = stage[:].bitcast(F32).rearrange("p (k c) -> p k c", k=KT)
        x2T = tuple(stage[:, i * KT * S:(i + 1) * KT * S].rearrange("p (k t) -> p k t", k=KT) for i in range(2))
        Wqkv, Wo, Wb, Lb = (pair("Wqkv", [P, KT, QW + 2 * KW]), pair("Wo", [P, KT, D]), pair("Wb", [P, KT, D]), pair("Lb", [P, D]))
        Lr = sb("Lr", [P, KT, P + E])
        b_base, b_router, invk = sb("b_base", [P, D]), sb("b_router", [P, E]), sb("invk", [P, E])
        cos, sin, mask, ident = sb("cos", [P, TT, HD]), sb("sin", [P, TT, HD]), sb("mask", [P, S]), sb("ident", [P, P])
        ident_r, mhalf = sb("ident_r", [P, P], F32R), sb("mhalf", [P, 1])
        xT32, xT, X = sb("xT32", [P, KT, S]), pair("xT", [P, KT, S]), sb("X", [P, TT, D])
        rq, tq = sb("rq", [P, H, HD]), sb("tq", [P, H, HD])
        rk, tk, v32 = sb("rk", [P, TT, G, HD]), sb("tk", [P, TT, G, HD]), sb("v32", [P, TT, G, HD])
        Qs = sb("Qs", [P, TT, H, 2, 2, HD], F32R)
        Ks = sb("Ks", [P, TT, G, 4, 2, HD], F32R)
        QT = sb("QT", [P, NP, S], F32R)
        KZ = sb("KZ", [P, G, 2, S], F32R)
        V = sb("V", [P, TT, G, VC])
        p, nmax = sb("p", [P, 2, 2, 3 * P]), sb("nmax", [P, 2, 4])
        pT = sb("pT", [P, 2, 6 * P])
        ot, rinv, Oat = sb("ot", [P, S]), sb("rinv", [P, TT, 4]), sb("Oat", [P, TT, H, HD])
        OT, x1T32, x1T = pair("OT", [P, KT, S]), sb("x1T32", [P, KT, S]), pair("x1T", [P, KT, S])
        stats, mv = sb("stats", [P, TT, 6]), sb("mv", [P, TT, 2])
        veps, rstd = sb("veps", [P, TT]), sb("rstd", [P, TT])
        z, c0, c1, c2, tau = sb("z", [P, TT, E]), sb("c0", [P, TT, 12]), sb("c1", [P, TT, 12]), sb("c2", [P, TT, 12]), sb("tau", [P, TT])
        c3, hw, hwT = sb("c3", [P, TT, E]), sb("hw", [P, TT, P]), pair("hwT", [P, S])
        bank = ctx.enter_context(nc.psum_tensor("l0_bank", [P, 8, D], F32))
        OB, F0, F1, F2 = 4, 5, 6, 7

        dve_zeroed, consts_in, xt_in, x_in, raw_in, zeroed = (
            sem("dve_zeroed"), sem("consts_in"), sem("xt_in"), sem("x_in"), sem("raw_in"), sem("zeroed"))
        w_hi, w_lo, ident_set, xs_hi, xs_lo, q_done = (
            sem("w_hi"), sem("w_lo"), sem("ident_set"), sem("xs_hi"), sem("xs_lo"), sem("q_done"))
        kv_done, q_parts, k_parts, v_staged, q_rot, k_rot = (
            sem("kv_done"), sem("q_parts"), sem("k_parts"), sem("v_staged"), sem("q_rot"), sem("k_rot"))
        q_hi, q_lo, k_hi, k_lo, q_turned, k_turned = (
            sem("q_hi"), sem("q_lo"), sem("k_hi"), sem("k_lo"), sem("q_turned"), sem("k_turned"))
        qt_done, kz_top, kz_bottom, v_set, s_done, masked = (
            sem("qt_done"), sem("kz_top"), sem("kz_bottom"), sem("v_set"), sem("s_done"), sem("masked"))
        exp_done, p_turned, pT0_done, pT1_done, pv_done, ot_done = (
            sem("exp_done"), sem("p_turned"), sem("pT0_done"), sem("pT1_done"), sem("pv_done"), sem("ot_done"))
        o_turned, rinv_done, o_out, oT_turned, oT_hi, oT_lo = (
            sem("o_turned"), sem("rinv_done"), sem("o_out"), sem("oT_turned"), sem("oT_hi"), sem("oT_lo"))
        r_done, added, stats_done, aggr_done, veps_done, rstd_done = (
            sem("r_done"), sem("added"), sem("stats_done"), sem("aggr_done"), sem("veps_done"), sem("rstd_done"))
        normed, x1_turned, x1_32, x1_hi, x1_lo, b_added = (
            sem("normed"), sem("x1_turned"), sem("x1_32"), sem("x1_hi"), sem("x1_lo"), sem("b_added"))
        lr_done, routing_steps, hw_done, hw_turned, hwT_hi, hwT_lo = (
            sem("lr_done"), sem("routing_steps"), sem("hw_done"), sem("hw_turned"), sem("hwT_hi"), sem("hwT_lo"))
        z_done, x2_turned, x2_hi, x2_lo, x2_stored, x2T_stored = (
            sem("z_done"), sem("x2_turned"), sem("x2_hi"), sem("x2_lo"), sem("x2_stored"), sem("x2T_stored"))
        block = ctx.enter_context(nc.Block())

        def wait(eng, semaphore, value, total=None):
            if isinstance(value, int):
                if total is not None:
                    value = min(value, total)
                if value <= 0:
                    return
            eng.wait_ge(semaphore, value)

        def tok(t):
            return slice(t * P, (t + 1) * P)

        def kt_view(ap):
            return ap.rearrange("p (k t) -> p k t", k=KT)

        @block.sync
        def _(sp):
            sp.dma_start(xT32[:], xT_in[:, 0]).then_inc(xt_in, 16)
            sp.dma_start(raw, w_qkv).then_inc(raw_in, 16)
            for t, src in ((ident, ident_t), (cos, cos_t), (sin, sin_t), (mask, mask_t), (invk, inv_k),
                           (b_router, b_router_row.partition_broadcast(P)), (b_base, b_base_row.partition_broadcast(P)),
                           (Lr, w_lr)):
                sp.dma_start(t[:], src).then_inc(consts_in, 16)
            sp.dma_start(X[:], x_in_t[:, 0]).then_inc(x_in, 16)
            sp.wait_ge(xs_lo, 1)
            sp.dma_start(xT32[:], xT_in[:, 1]).then_inc(xt_in, 16)
            for i, (src, n) in enumerate(((w_o, D), (w_base, D))):
                sp.wait_ge(w_lo, i + 1)
                sp.dma_start(raw[:, :, 0:n], src).then_inc(raw_in, 16)
            sp.wait_ge(w_lo, 3)
            sp.dma_start(raw[:, 0, 0:D], w_lb).then_inc(raw_in, 16)

            def batch(m, load_x, load_xt):
                if load_xt is not None:
                    sp.wait_ge(xs_lo, load_xt)
                    sp.dma_start(xT32[:], xT_in[:, load_xt]).then_inc(xt_in, 16)
                for t in range(TT):
                    sp.wait_ge(normed, 4 * m + 3 + t)
                    sp.dma_start(x2[:, m, t], X[:, t]).then_inc(x2_stored, 16)
                if load_x is not None:
                    sp.wait_ge(x2_turned, 2 * m + 2)
                    sp.wait_ge(x2_stored, 32 * m + 32)
                    sp.dma_start(X[:], x_in_t[:, load_x]).then_inc(x_in, 16)
                sp.wait_ge(x2_lo, 2 * m + 2)
                sp.dma_start(x2T_hi[:, m], x2T[0].bitcast(F32)).then_inc(x2T_stored, 16)
                sp.dma_start(x2T_lo[:, m], x2T[1].bitcast(F32)).then_inc(x2T_stored, 16)

            sp.wait_ge(xs_lo, 2)
            sp.dma_start(xT32[:], xT_in[:, 2]).then_inc(xt_in, 16)
            batch(0, 1, 3)
            with sp.Fori(1, B - 3) as m:
                batch(m, m + 1, m + 3)
            batch(B - 3, B - 2, None)
            batch(B - 2, B - 1, None)
            batch(B - 1, None, None)
            sp.wait_ge(x2_stored, 32 * B)
            sp.wait_ge(x2T_stored, 32 * B)

        @block.tensor
        def _(pe):
            def queries(n, t, part):
                if part == 1:
                    pass
                elif t == 0:
                    wait(pe, xs_lo, n + 1)
                    wait(pe, kz_top, 4 * n - 2)
                    wait(pe, kz_bottom, 4 * n - 2)
                else:
                    wait(pe, q_parts, 2 * n + 1)
                for kt in (2 * part, 2 * part + 1):
                    mm = product(pe, bank[:, F0, :], halves(xT, slice(None), kt, tok(t)),
                                 halves(Wqkv, slice(None), kt, slice(0, QW)), kt == 0, kt == KT - 1)
                if part == 1:
                    mm.then_inc(q_done, 1)

            def keys_values(n, t):
                if t == 0:
                    wait(pe, qt_done, 8 * n - 1)
                if True:
                    for kt in range(KT):
                        mm = product(pe, bank[:, F1, t * S:(t + 1) * S], halves(xT, slice(None), kt, tok(t)),
                                     halves(Wqkv, slice(None), kt, slice(QW, QW + 2 * KW)), kt == 0, kt == KT - 1)
                if t == 1:
                    mm.then_inc(kv_done, 1)

            def turn_queries(n, k, t):
                b = {0: F2, 1: F2, 2: F0, 3: (F1, F2)[t]}[k] if k == 3 else (F2 if k < 2 else F0)
                wait(pe, q_lo, 2 * n + 1 + t)
                if k == 0 and t == 0:
                    wait(pe, kz_top, 4 * n)
                    wait(pe, kz_bottom, 4 * n)
                    wait(pe, oT_lo, 2 * n - 2)
                elif k == 2 and t == 0:
                    wait(pe, hwT_lo, n - 1)
                    wait(pe, kz_top, 4 * n + 1)
                    wait(pe, kz_bottom, 4 * n + 1)
                elif k == 3:
                    wait(pe, x2_lo, 2 * n - 3 + t)
                else:
                    wait(pe, qt_done, 8 * n + 2 * k + t)
                for j in range(4):
                    i = 4 * k + j
                    mm = pe.transpose(bank[:, b, tok(j)].bitcast(F32R),
                                      Qs[:, t, 2 * i:2 * i + 2].rearrange("p h a c d -> p (h a c d)"), ident_r[:])
                mm.then_inc(q_turned, 1)

            def turn_keys(n, k, t):
                b = F0 if k == 0 else F2
                wait(pe, k_lo, n + 1)
                if (k, t) == (1, 1):
                    wait(pe, kz_top, 4 * n + 3)
                    wait(pe, kz_bottom, 4 * n + 3)
                elif (k, t) == (0, 0):
                    wait(pe, x1_hi, 2 * n - 3)
                    wait(pe, q_parts, 2 * n + 2)
                else:
                    wait(pe, qt_done, 8 * n + {(0, 1): 6, (1, 0): 8}[k, t])
                for j in range(4):
                    g = 4 * k + j
                    mm = pe.transpose(bank[:, b, tok(j)].bitcast(F32R), Ks[:, t, g].rearrange("p a c d -> p (a c d)"), ident_r[:])
                mm.then_inc(k_turned, 1)

            def scores(n, i):
                N, st, g = NP * n + i, i % 2, i // 2
                if i % 4 == 0:
                    wait(pe, qt_done, 8 * n + 2 * (i // 4) + 2)
                if i % 8 == 0:
                    wait(pe, kz_top, 4 * n + 2 * (i // 8) + 2)
                    wait(pe, kz_bottom, 4 * n + 2 * (i // 8) + 2)
                wait(pe, pT0_done, N - 1)
                wait(pe, pT1_done, N - 1)
                pe.matmul(bank[:, 2 * st, :], QT[:, i, P:S], KZ[:, g], start=True, stop=True)
                pe.matmul(bank[:, 2 * st + 1, 0:S], QT[:, i, 0:P], KZ[:, g, :, 0:P], start=True, stop=True).then_inc(s_done, 1)

            def turn(n, i):
                N, st = NP * n + i, i % 2
                wait(pe, exp_done, 4 * N + 4)
                for h in range(2):
                    pe.transpose(bank[:, 2 * st, h * S:h * S + P], p[:, st, h, 2 * P:3 * P], ident[:])
                    mm = pe.transpose(bank[:, 2 * st, h * S + P:(h + 1) * S], p[:, st, h, 0:P], ident[:])
                mm.then_inc(p_turned, 1)
                for h in range(2):
                    mm = pe.transpose(bank[:, 2 * st + 1, h * P:(h + 1) * P], p[:, st, h, P:2 * P], ident[:])
                mm.then_inc(p_turned, 1)

            def weigh(n, i):
                N, st, g = NP * n + i, i % 2, i // 2
                wait(pe, pT0_done, N + 1)
                wait(pe, pT1_done, N + 1)
                if i == 0:
                    wait(pe, v_set, n + 1)
                if i % 2 == 0:
                    wait(pe, o_out, G * n + g)
                for h in range(2):
                    j = 2 * (i % 2) + h
                    pe.matmul(bank[VC * j:VC * (j + 1), OB, 0:S], V[:, 0, g], pT[:, st, h * S:(h + 1) * S], start=True, stop=False)
                for h in range(2):
                    j = 2 * (i % 2) + h
                    mm = pe.matmul(bank[VC * j:VC * (j + 1), OB, P:S], V[:, 1, g], pT[:, st, 4 * P + h * P:4 * P + (h + 1) * P],
                                   start=False, stop=True)
                mm.then_inc(pv_done, 1)

            def turn_group(n, g):
                wait(pe, ot_done, G * n + g + 1)
                for t in range(TT):
                    mm = pe.transpose(bank[:, OB, S + t * P:S + (t + 1) * P], ot[:, tok(t)], ident[:])
                mm.then_inc(o_turned, 1)

            def turn_outputs(m, t):
                wait(pe, o_out, G * m + G)
                if t == 0:
                    wait(pe, k_parts, m + 3, B)
                    wait(pe, v_staged, m + 3, B)
                else:
                    wait(pe, kz_top, 4 * m + 8, 4 * B)
                    wait(pe, kz_bottom, 4 * m + 8, 4 * B)
                o = Oat[:, t].rearrange("p h d -> p (h d)")
                for kt in range(KT):
                    mm = pe.transpose(bank[:, (F1, F2)[t], tok(kt)], o[:, tok(kt)], ident[:])
                mm.then_inc(oT_turned, 1)

            def attention_rows(m, t, part):
                if part == 0:
                    wait(pe, oT_lo, 2 * m + 1 + t)
                    wait(pe, w_lo, 2)
                if t == 0 and part == 0:
                    wait(pe, q_parts, 2 * m + 6, 2 * B)
                for kt in (2 * part, 2 * part + 1):
                    mm = product(pe, bank[:, (F0, F1)[t], :], halves(OT, slice(None), kt, tok(t)), halves(Wo, slice(None), kt),
                                 kt == 0, kt == KT - 1)
                if part == 1:
                    mm.then_inc(r_done, 1)

            def turn_x1(m, t):
                wait(pe, normed, 4 * m + 1 + t)
                for kt in range(KT):
                    mm = pe.transpose(bank[:, (F0, F1)[t], tok(kt)], X[:, t, tok(kt)], ident[:])
                mm.then_inc(x1_turned, 1)

            def lora_down(m):
                wait(pe, x1_32, 2 * m + 2)
                wait(pe, x1_hi, 2 * m + 1)
                wait(pe, kz_top, 4 * m + 9, 4 * B)
                wait(pe, kz_bottom, 4 * m + 9, 4 * B)
                for t in range(TT):
                    for kt in range(KT):
                        mm = pe.matmul(bank[:, F0, t * S:t * S + P + E], x1T32[:, kt, tok(t)], Lr[:, kt], start=kt == 0, stop=kt == KT - 1)
                mm.then_inc(lr_done, 1)

            def base(m, t, part):
                if part == 0:
                    wait(pe, w_lo, 3)
                    wait(pe, x1_hi, 2 * m + 2)
                    wait(pe, x1_lo, 2 * m + 1 + t)
                if t == 1 and part == 0:
                    wait(pe, qt_done, 8 * m + 20, 8 * B)
                for kt in (2 * part, 2 * part + 1):
                    mm = product(pe, bank[:, (F1, F2)[t], :], halves(x1T, slice(None), kt, tok(t)), halves(Wb, slice(None), kt), kt == 0, False)

            def turn_weighted(m):
                wait(pe, hw_done, m + 1)
                for t in range(TT):
                    mm = pe.transpose(bank[:, F0, tok(t)], hw[:, t], ident[:])
                mm.then_inc(hw_turned, 1)

            def lora_up(m, t):
                wait(pe, hwT_lo, m + 1)
                wait(pe, w_lo, 4)
                product(pe, bank[:, (F1, F2)[t], :], halves(hwT, slice(None), tok(t)), halves(Lb, slice(None)), False, True).then_inc(z_done, 1)

            def turn_x2(m, t):
                wait(pe, normed, 4 * m + 3 + t)
                for kt in range(KT):
                    mm = pe.transpose(bank[:, (F1, F2)[t], tok(kt)], X[:, t, tok(kt)], ident[:])
                mm.then_inc(x2_turned, 1)

            def tail(m, i):
                if i == 3:
                    turn_outputs(m, 0), turn_outputs(m, 1)
                if i == 4:
                    attention_rows(m, 0, 0)
                if i == 5:
                    attention_rows(m, 0, 1), attention_rows(m, 1, 0)
                if i == 6:
                    attention_rows(m, 1, 1)
                if i == 7:
                    turn_x1(m, 0)
                if i == 8:
                    turn_x1(m, 1)
                if i == 9:
                    lora_down(m), base(m, 0, 0)
                if i == 10:
                    base(m, 0, 1), base(m, 1, 0)
                if i == 11:
                    turn_weighted(m), base(m, 1, 1)
                if i == 12:
                    lora_up(m, 0), lora_up(m, 1)
                if i == 15:
                    turn_x2(m, 0), turn_x2(m, 1)

            def head(n, i):
                if i == 0:
                    queries(n, 0, 0)
                if i == 1:
                    queries(n, 0, 1), keys_values(n, 0)
                if i == 2:
                    keys_values(n, 1), queries(n, 1, 0)
                if i == 3:
                    queries(n, 1, 1)
                for at, k, t in ((5, 0, 0), (6, 0, 1), (7, 1, 0), (8, 1, 1), (13, 2, 0), (14, 2, 1)):
                    if at == i:
                        turn_queries(n, k, t)
                if i == 8:
                    turn_keys(n, 0, 0)
                if i == 15:
                    turn_keys(n, 0, 1)

            def batch(b, heads, tails):
                for i in range(NP):
                    prev = (b, i - 1) if i else (b - 1, NP - 1)
                    some = i > 0 or not (isinstance(b, int) and b == 0)
                    scores(b, i)
                    if some:
                        turn(*prev)
                    if i == 0:
                        turn_queries(b, 3, 0), turn_queries(b, 3, 1)
                    if i == 1:
                        turn_keys(b, 1, 0)
                    if i == 2:
                        turn_keys(b, 1, 1)
                    if i % 2 == 1 and i > 1:
                        turn_group(b, (i - 3) // 2)
                    if i == 1 and not (isinstance(b, int) and b == 0):
                        turn_group(b - 1, G - 1)
                    if heads:
                        head(b + 1, i)
                    if tails:
                        tail(b - 1, i)
                    if some:
                        weigh(*prev)

            wait(pe, consts_in, 16 * 8)
            wait(pe, ident_set, 1)
            wait(pe, w_lo, 1)
            for i in range(NP):
                head(0, i)
            batch(0, True, False)
            batch(1, True, True)
            with pe.Fori(2, B - 1) as b:
                batch(b, True, True)
            batch(B - 1, False, True)
            turn(B - 1, NP - 1)
            weigh(B - 1, NP - 1)
            turn_group(B - 1, G - 1)
            for i in range(NP):
                tail(B - 1, i)

        @block.scalar
        def _(act):
            def split_x(n):
                wait(act, xt_in, 16 * n + 16)
                wait(act, q_done, 2 * n)
                wait(act, kv_done, n)
                act.activation(xT[0][:], xT32[:], ACT.Copy).then_inc(xs_hi, 1)

            def stack_queries(n, t):
                wait(act, q_rot, 2 * n + 1 + t)
                wait(act, q_turned, 8 * n)
                act.activation(Qs[:, t, :, 0], rq[:].unsqueeze(2).to_broadcast([P, H, 2, HD]), ACT.Copy).then_inc(q_hi, 1)

            def stack_keys(n):
                wait(act, k_rot, n + 1)
                wait(act, k_turned, 4 * n)
                for t in range(TT):
                    act.activation(Ks[:, t, :, :, 0], rk[:, t].unsqueeze(2).to_broadcast([P, G, 4, HD]), ACT.Copy).then_inc(k_hi, 1)

            def stage_values(n):
                wait(act, kv_done, n + 1)
                wait(act, v_set, n)
                v = bank[:, F1, :].rearrange("p (t c) -> p t c", t=TT)[:, :, KW:]
                act.activation(v32[:].rearrange("p t g d -> p t (g d)"), v, ACT.Copy).then_inc(v_staged, 1)

            def set_values(n):
                wait(act, v_staged, n + 1)
                wait(act, pv_done, NP * n)
                act.activation(V[:, :, :, 0:HD], v32[:], ACT.Copy).then_inc(v_set, 1)

            def queries_turned(n, k, t):
                b = (F1, F2)[t] if k == 3 else (F2 if k < 2 else F0)
                wait(act, q_turned, 8 * n + 2 * k + t + 1)
                wait(act, s_done, NP * n - NP + 4 * k + 4 if not (isinstance(n, int) and n == 0) else 0)
                act.activation(QT[:, 4 * k:4 * k + 4, tok(t)], bank[:, b, :].rearrange("p (j t) -> p j t", j=4), ACT.Copy).then_inc(qt_done, 1)

            def keys_turned(n, k, t):
                b = F0 if k == 0 else F2
                wait(act, k_turned, 4 * n + 2 * k + t + 1)
                wait(act, s_done, NP * n - NP + 8 * k + 8 if not (isinstance(n, int) and n == 0) else 0)
                act.activation(KZ[0:64, 4 * k:4 * k + 4, 0, tok(t)], bank[0:64, b, :].rearrange("p (j t) -> p j t", j=4),
                               ACT.Copy).then_inc(kz_top, 1)

            def exponentials(n, i):
                N, st = NP * n + i, i % 2
                for j in range(4):
                    h = j // 2
                    wait(act, masked, 4 * N + j + 1)
                    t = p[:, st, h, 0:2 * P] if j % 2 == 0 else p[:, st, h, 2 * P:]
                    act.activation(t, t, ACT.Exp, bias=nmax[:, st, j:j + 1], scale=-1.0).then_inc(exp_done, 1)

            def turned(n, i):
                N, st = NP * n + i, i % 2
                wait(act, p_turned, 2 * N + 1)
                wait(act, pv_done, N - 1)
                act.activation(pT[:, st, 0:4 * P], bank[:, 2 * st, :], ACT.Copy).then_inc(pT0_done, 1)

            def group(n, g):
                wait(act, pv_done, NP * n + 2 * g + 2)
                wait(act, o_turned, G * n + g)
                act.activation(ot[:], bank[:, OB, 0:S], ACT.Copy).then_inc(ot_done, 1)

            def high(dst, count, sem_in, value, sem_out, b, t, free):
                wait(act, sem_in, value)
                for f in free:
                    wait(act, *f)
                act.activation(dst[:, :, tok(t)], kt_view(bank[:, b, :]), ACT.Copy).then_inc(sem_out, 1)

            def tail(m, i):
                if i == 3:
                    for t in range(TT):
                        high(OT[0], 0, oT_turned, 2 * m + 1 + t, oT_hi, (F1, F2)[t], t, [(r_done, 2 * m)])
                if i in (7, 8):
                    t = i - 7
                    high(x1T32, 0, x1_turned, 2 * m + 1 + t, x1_32, (F0, F1)[t], t, [(lr_done, m), (x1_lo, 2 * m)])
                    high(x1T[0], 0, x1_turned, 2 * m + 1 + t, x1_hi, (F0, F1)[t], t, [(z_done, 2 * m)])
                if i == 11:
                    wait(act, hw_turned, m + 1)
                    wait(act, z_done, 2 * m)
                    act.activation(hwT[0][:], bank[:, F0, 0:S], ACT.Copy).then_inc(hwT_hi, 1)
                if i == 15:
                    for t in range(TT):
                        high(x2T[0], 0, x2_turned, 2 * m + 1 + t, x2_hi, (F1, F2)[t], t, [(x2T_stored, 32 * m), (w_lo, 4)])

            def head(n, i):
                if i == 2:
                    stack_queries(n, 0), stage_values(n)
                if i == 3:
                    stack_keys(n)
                if i == 4:
                    stack_queries(n, 1)
                for at, k, t in ((5, 0, 0), (6, 0, 1), (7, 1, 0), (8, 1, 1), (13, 2, 0), (14, 2, 1)):
                    if at == i:
                        queries_turned(n, k, t)
                if i == 8:
                    keys_turned(n, 0, 0)
                if i == 15:
                    keys_turned(n, 0, 1)
                if i == 10 and not (isinstance(n, int) and n + 1 >= B):
                    split_x(n + 1)

            def batch(b, heads, tails):
                for i in range(NP):
                    prev = (b, i - 1) if i else (b - 1, NP - 1)
                    some = i > 0 or not (isinstance(b, int) and b == 0)
                    if i % 2 == 1 and i > 1:
                        group(b, (i - 3) // 2)
                    if i == 1 and not (isinstance(b, int) and b == 0):
                        group(b - 1, G - 1)
                    if i == 1:
                        set_values(b)
                    if some:
                        turned(*prev)
                    exponentials(b, i)
                    if i == 0:
                        queries_turned(b, 3, 0), queries_turned(b, 3, 1)
                    if i == 1:
                        keys_turned(b, 1, 0)
                    if i == 2:
                        keys_turned(b, 1, 1)
                    if heads:
                        head(b + 1, i)
                    if tails:
                        tail(b - 1, i)

            split_x(0)
            wait(act, raw_in, 16)
            act.activation(Wqkv[0][:], raw, ACT.Copy).then_inc(w_hi, 1)
            wait(act, consts_in, 16 * 8)
            act.activation(ident_r[:], ident[:], ACT.Copy).then_inc(ident_set, 1)
            for i in range(3):
                head(0, i)
            wait(act, raw_in, 32)
            act.activation(Wo[0][:], raw[:, :, 0:D], ACT.Copy).then_inc(w_hi, 1)
            for i in range(3, NP):
                head(0, i)
            wait(act, raw_in, 48)
            act.activation(Wb[0][:], raw[:, :, 0:D], ACT.Copy).then_inc(w_hi, 1)
            wait(act, raw_in, 64)
            act.activation(Lb[0][:], raw[:, 0, 0:D], ACT.Copy).then_inc(w_hi, 1)
            batch(0, True, False)
            batch(1, True, True)
            with act.Fori(2, B - 2) as b:
                batch(b, True, True)
            batch(B - 2, True, True)
            batch(B - 1, False, True)
            turned(B - 1, NP - 1)
            group(B - 1, G - 1)
            for i in range(NP):
                tail(B - 1, i)

        @block.vector
        def _(dve):
            def rotate_queries(n, t):
                wait(dve, q_done, 2 * n + 1 + t)
                wait(dve, q_lo, 2 * n + t)
                x = bank[:, F0, :].rearrange("p (h d) -> p h d", h=H)
                dve.tensor_tensor(rq[:], x, cos[:, t].unsqueeze(1).to_broadcast([P, H, HD]), ALU.mult)
                dve.tensor_tensor(tq[:, :, 0:HP], x[:, :, HP:], sin[:, t, 0:HP].unsqueeze(1).to_broadcast([P, H, HP]), ALU.mult)
                dve.tensor_tensor(tq[:, :, HP:], x[:, :, 0:HP], sin[:, t, HP:].unsqueeze(1).to_broadcast([P, H, HP]), ALU.mult).then_inc(q_parts, 1)

            def rotate_keys(n):
                wait(dve, kv_done, n + 1)
                wait(dve, v_staged, n + 1)
                wait(dve, k_lo, n)
                for t in range(TT):
                    x = bank[:, F1, t * S:t * S + KW].rearrange("p (h d) -> p h d", h=G)
                    dve.tensor_tensor(rk[:, t], x, cos[:, t].unsqueeze(1).to_broadcast([P, G, HD]), ALU.mult)
                    dve.tensor_tensor(tk[:, t, :, 0:HP], x[:, :, HP:], sin[:, t, 0:HP].unsqueeze(1).to_broadcast([P, G, HP]), ALU.mult)
                    mm = dve.tensor_tensor(tk[:, t, :, HP:], x[:, :, 0:HP], sin[:, t, HP:].unsqueeze(1).to_broadcast([P, G, HP]), ALU.mult)
                mm.then_inc(k_parts, 1)

            def keys_turned(n, k, t):
                b = F0 if k == 0 else F2
                wait(dve, k_turned, 4 * n + 2 * k + t + 1)
                wait(dve, kz_top, 4 * n + 2 * k + t + 1)
                wait(dve, s_done, NP * n - NP + 8 * k + 8 if not (isinstance(n, int) and n == 0) else 0)
                dve.tensor_copy(KZ[64:128, 4 * k:4 * k + 4, 1, tok(t)], bank[64:128, b, :].rearrange("p (j t) -> p j t", j=4))\
                    .then_inc(kz_bottom, 1)

            def mask_scores(n, i):
                N, st = NP * n + i, i % 2
                for j in range(4):
                    h = j // 2
                    if j % 2 == 0:
                        t, src, msk = p[:, st, h, 0:2 * P], bank[:, 2 * st, h * S:(h + 1) * S], mask[:]
                    else:
                        t, src, msk = p[:, st, h, 2 * P:], bank[:, 2 * st + 1, h * P:(h + 1) * P], mask[:, P:S]
                    dve.tensor_tensor_reduce(t, src, msk, -SCALE, BIG, ALU.add, ALU.min, nmax[:, st, j:j + 1]).then_inc(masked, 1)

            def turned(n, i, N_scores, also=None):
                N, st = NP * n + i, i % 2
                wait(dve, p_turned, 2 * N + 2)
                wait(dve, pv_done, N - 1)
                if N_scores is not None:
                    wait(dve, s_done, N_scores + 1)
                if also is not None:
                    wait(dve, *also)
                dve.tensor_scalar(pT[:, st, 4 * P:6 * P], bank[:, 2 * st + 1, 0:S], 1.0, None, ALU.mult).then_inc(pT1_done, 1)

            def group(n, g):
                wait(dve, o_turned, G * n + g + 1)
                wait(dve, oT_turned, 2 * n)
                wait(dve, o_out, G * n + g)
                o = bank[:, OB, S:].rearrange("p (t j c) -> p t j c", t=TT, j=4)
                dve.reciprocal(rinv[:], o[:, :, :, HD]).then_inc(rinv_done, 1)
                wait(dve, rinv_done, G * n + g + 1)
                dve.tensor_tensor(Oat[:, :, 4 * g:4 * g + 4], o[:, :, :, 0:HD], rinv[:].unsqueeze(3).to_broadcast([P, TT, 4, HD]), ALU.mult).then_inc(o_out, 1)

            def residual(m, k, done, b):
                t, c = k % 2, 4 * m + k
                wait(dve, *done)
                if k < 2:
                    wait(dve, x_in, 16 * m + 16)
                else:
                    wait(dve, b_added, 2 * m + 1 + t)
                dve.tensor_tensor(X[:, t], bank[:, b, :], X[:, t], ALU.add).then_inc(added, 1)
                wait(dve, added, c + 1)
                dve.bn_stats(stats[:, t], X[:, t]).then_inc(stats_done, 1)

            def variance(m, k):
                t, c = k % 2, 4 * m + k
                if isinstance(m, int):
                    wait(dve, stats_done, c + 1)
                dve.bn_aggr(mv[:, t], stats[:, t]).then_inc(aggr_done, 1)
                wait(dve, aggr_done, c + 1)
                dve.tensor_scalar(veps[:, t:t + 1], mv[:, t, 1:2], EPS, None, ALU.add).then_inc(veps_done, 1)

            def ln_finish(m, k):
                t, c = k % 2, 4 * m + k
                wait(dve, rstd_done, c + 1)
                dve.tensor_scalar(X[:, t], X[:, t], mv[:, t, 0:1], rstd[:, t:t + 1], ALU.subtract, ALU.mult).then_inc(normed, 1)

            def low(dst, b, t, sem_in, sem_out, value, free=()):
                wait(dve, sem_in, value)
                for f in free:
                    wait(dve, *f)
                dve.tensor_tensor(dst[1][:, :, tok(t)], kt_view(bank[:, b, :]), dst[0][:, :, tok(t)].bitcast(F32), ALU.subtract).then_inc(sem_out, 1)

            def logits(m):
                wait(dve, lr_done, m + 1)
                wait(dve, hw_turned, m)
                lr = bank[:, F0, :].rearrange("p (t c) -> p t c", t=TT)
                dve.tensor_tensor(z[:], lr[:, :, P:P + E], b_router[:].unsqueeze(1).to_broadcast([P, TT, E]), ALU.add).then_inc(routing_steps, 1)

            def sparsemax(m):
                c = [12 * m + 1]

                def step(ins):
                    ins.then_inc(routing_steps, 1)
                    c[0] = c[0] + 1
                    wait(dve, routing_steps, c[0])

                lr = bank[:, F0, :].rearrange("p (t c) -> p t c", t=TT)
                if isinstance(m, int):
                    wait(dve, routing_steps, c[0])
                for t in range(TT):
                    ins = dve.max(out=c0[:, t, 4:12], in_=z[:, t])
                step(ins)
                step(dve.tensor_tensor(c1[:, :, 4:12], c0[:, :, 4:12], c0[:, :, 3:11], ALU.add))
                step(dve.tensor_tensor(c2[:, :, 4:12], c1[:, :, 4:12], c1[:, :, 2:10], ALU.add))
                step(dve.tensor_tensor(c3[:], c2[:, :, 4:12], c2[:, :, 0:8], ALU.add))
                step(dve.tensor_scalar(c3[:], c3[:], 1.0, None, ALU.subtract))
                step(dve.tensor_tensor(c3[:], c3[:], invk[:].unsqueeze(1).to_broadcast([P, TT, E]), ALU.mult))
                step(dve.tensor_reduce(tau[:], c3[:], AX.X, ALU.max))
                step(dve.tensor_tensor(z[:], z[:], tau[:].unsqueeze(2).to_broadcast([P, TT, E]), ALU.subtract))
                step(dve.tensor_scalar(z[:], z[:], 0.0, None, ALU.max))
                for t in range(TT):
                    step(dve.tensor_tensor(hw[:, t].rearrange("p (e r) -> p e r", e=E), lr[:, t, 0:P].rearrange("p (e r) -> p e r", e=E),
                                           z[:, t].unsqueeze(2).to_broadcast([P, E, R]), ALU.mult))
                assert not isinstance(m, int) or c[0] == 12 * m + 12
                dve.tensor_scalar(z[:], z[:], 0.0, None, ALU.max).then_inc(hw_done, 1)

            def tail(m, i):
                if i == 3:
                    for t in range(TT):
                        low(OT, (F1, F2)[t], t, oT_hi, oT_lo, 2 * m + 1 + t)
                if i == 5:
                    residual(m, 0, (r_done, 2 * m + 1), F0)
                if i == 6:
                    variance(m, 0)
                    residual(m, 1, (r_done, 2 * m + 2), F1)
                    ln_finish(m, 0)
                if i == 7:
                    variance(m, 1)
                    ln_finish(m, 1)
                if i == 9:
                    logits(m)
                if i == 10:
                    sparsemax(m)
                if i == 11:
                    wait(dve, hwT_hi, m + 1)
                    dve.tensor_tensor(hwT[1][:], bank[:, F0, 0:S], hwT[0][:].bitcast(F32), ALU.subtract).then_inc(hwT_lo, 1)
                if i == 12:
                    residual(m, 2, (z_done, 2 * m + 1), F1)
                if i == 13:
                    variance(m, 2)
                    residual(m, 3, (z_done, 2 * m + 2), F2)
                    ln_finish(m, 2)
                if i == 14:
                    variance(m, 3)
                    ln_finish(m, 3)
                if i == 15:
                    for t in range(TT):
                        low(x2T, (F1, F2)[t], t, x2_hi, x2_lo, 2 * m + 1 + t)

            def head(n, i):
                if i == 1:
                    rotate_queries(n, 0)
                if i == 2:
                    rotate_keys(n)
                if i == 3:
                    rotate_queries(n, 1)
                if i == 8:
                    keys_turned(n, 0, 0)
                if i == 15:
                    keys_turned(n, 0, 1)

            def batch(b, heads, tails):
                for i in range(NP):
                    prev = (b, i - 1) if i else (b - 1, NP - 1)
                    some = i > 0 or not (isinstance(b, int) and b == 0)
                    if some:
                        k = {6: 0, 7: 1, 13: 2, 14: 3}.get(i)
                        also = None
                        if tails and k is not None:
                            also = (stats_done, 4 * (b - 1) + k + 1)
                        if tails and i == 10:
                            also = (routing_steps, 12 * (b - 1) + 1)
                        turned(*prev, NP * b + i, also)
                    else:
                        wait(dve, s_done, 1)
                    mask_scores(b, i)
                    if i % 2 == 1 and i > 1:
                        group(b, (i - 3) // 2)
                    if i == 1 and not (isinstance(b, int) and b == 0):
                        group(b - 1, G - 1)
                    if i == 1:
                        keys_turned(b, 1, 0)
                    if i == 2:
                        keys_turned(b, 1, 1)
                    if heads:
                        head(b + 1, i)
                    if tails:
                        tail(b - 1, i)

            for k, t in enumerate((c0, c1, c2)):
                ins = dve.memset(t[:], 0.0)
            wait(dve, consts_in, 16 * 8)
            ins = dve.memset(tau[:], 0.0)
            ins.then_inc(dve_zeroed, 1)
            wait(dve, dve_zeroed, 1)
            for i in range(NP):
                head(0, i)
            batch(0, True, False)
            batch(1, True, True)
            with dve.Fori(2, B - 1) as b:
                batch(b, True, True)
            batch(B - 1, False, True)
            turned(B - 1, NP - 1, None)
            group(B - 1, G - 1)
            for i in range(NP):
                tail(B - 1, i)

        @block.gpsimd
        def _(pool):
            def split_x(n):
                wait(pool, xs_hi, n + 1)
                pool.tensor_tensor(xT[1][:], xT32[:], xT[0][:].bitcast(F32), ALU.subtract).then_inc(xs_lo, 1)

            def add_queries(n, t):
                wait(pool, q_parts, 2 * n + 1 + t)
                pool.tensor_tensor(rq[:], rq[:], tq[:], ALU.add).then_inc(q_rot, 1)

            def stack_queries(n, t):
                wait(pool, q_hi, 2 * n + 1 + t)
                pool.tensor_tensor(Qs[:, t, :, 1], rq[:].unsqueeze(2).to_broadcast([P, H, 2, HD]), Qs[:, t, :, 0].bitcast(F32),
                                   ALU.subtract).then_inc(q_lo, 1)

            def add_keys(n):
                wait(pool, k_parts, n + 1)
                pool.tensor_tensor(rk[:], rk[:], tk[:], ALU.add).then_inc(k_rot, 1)

            def stack_keys(n):
                wait(pool, k_hi, 2 * n + 2)
                for t in range(TT):
                    ins = pool.tensor_tensor(Ks[:, t, :, :, 1], rk[:, t].unsqueeze(2).to_broadcast([P, G, 4, HD]),
                                             Ks[:, t, :, :, 0].bitcast(F32), ALU.subtract)
                ins.then_inc(k_lo, 1)

            def rescale(c):
                t = c[1] % 2
                wait(pool, veps_done, 4 * c[0] + c[1] + 1)
                pool.tensor_tensor(rstd[:, t:t + 1], veps[:, t:t + 1], mhalf[:], ALU.pow).then_inc(rstd_done, 1)

            def tail(m, i):
                if i == 6:
                    rescale((m, 0))
                if i == 7:
                    rescale((m, 1))
                if i in (7, 8):
                    t = i - 7
                    wait(pool, x1_hi, 2 * m + 1 + t)
                    wait(pool, z_done, 2 * m)
                    pool.tensor_tensor(x1T[1][:, :, tok(t)], x1T32[:, :, tok(t)], x1T[0][:, :, tok(t)].bitcast(F32), ALU.subtract).then_inc(x1_lo, 1)
                    wait(pool, x1_turned, 2 * m + 1 + t)
                    pool.tensor_tensor(X[:, t], X[:, t], b_base[:], ALU.add).then_inc(b_added, 1)
                if i == 13:
                    rescale((m, 2))
                if i == 14:
                    rescale((m, 3))

            def head(n, i):
                if i == 1:
                    add_queries(n, 0)
                if i == 2:
                    stack_queries(n, 0), add_keys(n)
                if i == 3:
                    stack_keys(n), add_queries(n, 1)
                if i == 4:
                    stack_queries(n, 1)
                if i == 10 and not (isinstance(n, int) and n + 1 >= B):
                    split_x(n + 1)

            def batch(b, heads, tails):
                for i in range(NP):
                    if heads:
                        head(b + 1, i)
                    if tails:
                        tail(b - 1, i)

            pool.memset(KZ[:].bitcast(F32), 0.0).then_inc(zeroed, 1)
            pool.memset(V[:], 0.0).then_inc(zeroed, 1)
            pool.memset(mhalf[:], -0.5).then_inc(zeroed, 1)
            wait(pool, zeroed, 3)
            pool.memset(V[:, :, :, HD:HD + 1], 1.0).then_inc(zeroed, 1)
            wait(pool, zeroed, 4)
            split_x(0)
            wait(pool, w_hi, 1)
            pool.tensor_tensor(Wqkv[1][:], raw, Wqkv[0][:].bitcast(F32), ALU.subtract).then_inc(w_lo, 1)
            for i in range(3):
                head(0, i)
            wait(pool, w_hi, 2)
            pool.tensor_tensor(Wo[1][:], raw[:, :, 0:D], Wo[0][:].bitcast(F32), ALU.subtract).then_inc(w_lo, 1)
            for i in range(3, NP):
                head(0, i)
            wait(pool, w_hi, 3)
            pool.tensor_tensor(Wb[1][:], raw[:, :, 0:D], Wb[0][:].bitcast(F32), ALU.subtract).then_inc(w_lo, 1)
            wait(pool, w_hi, 4)
            pool.tensor_tensor(Lb[1][:], raw[:, 0, 0:D], Lb[0][:].bitcast(F32), ALU.subtract).then_inc(w_lo, 1)
            batch(0, True, False)
            batch(1, True, True)
            with pool.Fori(2, B - 2) as b:
                batch(b, True, True)
            batch(B - 2, True, True)
            batch(B - 1, False, True)
            for i in range(NP):
                tail(B - 1, i)


def attention1(nc, x2, x2T_hi, x2T_lo, w_attn, cos_t, sin_t, mask_t, ident_t, XT, Y):
    G, HG, HD = 8, 4, 128
    STEPS = G * B
    SCALE = float(np.float32(1.0 / np.sqrt(HD)))
    KV, QO = 2 * KT * HD, KT * HG * HD
    with ExitStack() as ctx:
        def sb(name, shape, dt=F32):
            return ctx.enter_context(nc.sbuf_tensor("a1_" + name, shape, dt))

        def sem(name):
            return ctx.enter_context(nc.semaphore("a1_" + name))

        def pair(name, shape):
            return sb(name + "_hi", shape, F32R), sb(name + "_lo", shape, F32R)

        raw = sb("raw", [P, KV + QO])
        Wk, Wv = pair("Wk", [P, KT, HD]), pair("Wv", [P, KT, HD])
        Wq, Wo = pair("Wq", [P, KT, HG * HD]), pair("Wo", [P, HG, D])
        q32, q, tmp = sb("q32", [P, HG, S]), pair("q", [P, HG, S]), sb("tmp", [P, HG + 1, S])
        k32, k = sb("k32", [P, S]), pair("k", [P, S])
        vT, V = sb("vT", [P, S]), pair("V", [P, TT, HD])
        p = sb("p", [P, HG, 3 * P])
        pT = pair("pT", [P, 3 * HG * P])
        o = pair("o", [P, HG, S])
        cos, sin, mask, ident = sb("cos", [P, S]), sb("sin", [P, S]), sb("mask", [P, S]), sb("ident", [P, P])
        nmax, rsum, rinv = sb("nmax", [P, 2 * HG]), sb("rsum", [P, 2 * HG]), sb("rinv", [P, 2 * HG])
        bank = ctx.enter_context(nc.psum_tensor("a1_bank", [P, 8, D], F32))
        Q0, KVB, S0, SQ0, Y0 = 0, 2, 3, 5, 6

        consts_in, xt_in = sem("consts_in"), [sem(f"xt_in{i}") for i in range(3)]
        y_in, raw_in = sem("y_in"), sem("raw_in")
        w_hi, w_lo = sem("w_hi"), sem("w_lo")
        kv_done, q_done, v_turned = sem("kv_done"), sem("q_done"), sem("v_turned")
        s_done, p_turned, o_done, y_done = sem("s_done"), sem("p_turned"), sem("o_done"), sem("y_done")
        vT_copied, v_hi, k_hi, q_hi = sem("vT_copied"), sem("v_hi"), sem("k_hi"), sem("q_hi")
        exp_done, pT_hi, o_hi = sem("exp_done"), sem("pT_hi"), sem("o_hi")
        v_lo, masked, rinv_done, p_ready = sem("v_lo"), sem("masked"), sem("rinv_done"), sem("p_ready")
        k_parts, q_parts, pT_lo, o_lo, y_added = sem("k_parts"), sem("q_parts"), sem("pT_lo"), sem("o_lo"), sem("y_added")
        k_rot, q_rot, k_lo, q_lo = sem("k_rot"), sem("q_rot"), sem("k_lo"), sem("q_lo")

        block = ctx.enter_context(nc.Block())
        wa = w_attn

        kv_parts = ((Wk, 0, KV // 2), (Wv, KV // 2, KV))

        @block.sync
        def _(sp):
            sp.dma_start(raw[:], wa[:, 0, 0:KV + QO]).then_inc(raw_in, 16)
            for t, src in ((cos, cos_t), (sin, sin_t), (mask, mask_t), (ident, ident_t)):
                sp.dma_start(t[:], src).then_inc(consts_in, 16)
            for b in range(B):
                for half, src in zip(XT, (x2T_hi, x2T_lo)):
                    sp.dma_start(half[:, b].bitcast(F32), src[:, b]).then_inc(xt_in[min(b, 2)], 16)
            sp.dma_start(Y[:], x2).then_inc(y_in, 16)
            sp.wait_ge(w_lo, 2)
            sp.dma_start(raw[:, 0:QO], wa[:, 0, KV + QO:]).then_inc(raw_in, 16)
            with sp.Fori(1, G) as g:
                sp.wait_ge(w_lo, 3 * g)
                sp.dma_start(raw[:], wa[:, g, 0:KV + QO]).then_inc(raw_in, 16)
                sp.wait_ge(w_lo, 3 * g + 2)
                sp.dma_start(raw[:, 0:QO], wa[:, g, KV + QO:]).then_inc(raw_in, 16)

        @block.tensor
        def _(pe):
            def project(n, b, g):
                pe.wait_ge(w_lo, 3 * g + 2)
                xT = lambda kt: halves(XT, slice(None), b, kt)
                if not isinstance(n, int) or n >= 1:
                    pe.wait_ge(v_lo, n)
                for i, w in enumerate((Wk, Wv)):
                    for kt in range(KT):
                        mm = product(pe, bank[:, KVB, i * S:(i + 1) * S], halves(w, slice(None), kt), xT(kt),
                                     kt == 0, kt == KT - 1)
                mm.then_inc(kv_done, 1)
                for h in range(HG):
                    if h % 2 == 0 and (not isinstance(n, int) or n >= 2):
                        pe.wait_ge(o_lo, 2 * n - 3 + h // 2)
                    for kt in range(KT):
                        mm = product(pe, bank[:, Q0 + h // 2, h % 2 * S:(h % 2 + 1) * S],
                                     halves(Wq, slice(None), kt, slice(h * HD, (h + 1) * HD)), xT(kt),
                                     kt == 0, kt == KT - 1)
                    if h % 2:
                        mm.then_inc(q_done, 1)

            def scores(m):
                pe.wait_ge(k_parts, m + 1)
                pe.wait_ge(vT_copied, m + 1)
                for tt in range(TT):
                    mm = pe.transpose(bank[:, KVB, tt * P:(tt + 1) * P], vT[:, tt * P:(tt + 1) * P], ident[:])
                mm.then_inc(v_turned, 1)
                pe.wait_ge(k_lo, m + 1)
                pe.wait_ge(q_lo, 2 * m + 2)
                first = isinstance(m, int) and m == 0
                if not first:
                    pe.wait_ge(pT_lo, 3 * m)
                for h in range(HG):
                    mm = pe.matmul(bank[:, SQ0, h * P:(h + 1) * P], q32[:, h, 0:P], k32[:, 0:P], start=True, stop=True)
                mm.then_inc(s_done, 1)
                for h in range(HG):
                    mm = product(pe, bank[:, S0 + h // 2, h % 2 * S:(h % 2 + 1) * S],
                                 halves(q, slice(None), h, slice(P, S)), halves(k, slice(None)))
                    if h % 2:
                        mm.then_inc(s_done, 1)

            def turn(m):
                pe.wait_ge(p_ready, 8 * m + 8)
                for h in range(HG):
                    dst = bank[:, S0 + h // 2, h % 2 * S:(h % 2 + 1) * S]
                    pe.transpose(dst[:, 0:P], p[:, h, 2 * P:3 * P], ident[:])
                    mm = pe.transpose(dst[:, P:S], p[:, h, 0:P], ident[:])
                    if h % 2:
                        mm.then_inc(p_turned, 1)
                for h in range(HG):
                    mm = pe.transpose(bank[:, SQ0, h * P:(h + 1) * P], p[:, h, P:2 * P], ident[:])
                mm.then_inc(p_turned, 1)

            def rows(m, g):
                pe.wait_ge(w_lo, 3 * g + 3)
                pe.wait_ge(o_lo, 2 * m + 2)
                for tt in range(TT):
                    if not (isinstance(m, int) and m == 0):
                        pe.wait_ge(y_added, 2 * m - 1 + tt)
                    for h in range(HG):
                        mm = product(pe, bank[:, Y0 + tt, :], halves(o, slice(None), h, slice(tt * P, (tt + 1) * P)),
                                     halves(Wo, slice(None), h), h == 0, h == HG - 1)
                    mm.then_inc(y_done, 1)

            def values(m, last=False):
                pe.wait_ge(v_lo, m + 1)
                pe.wait_ge(pT_lo, 3 * m + 3)
                for i in range(2):
                    if not last:
                        pe.wait_ge(q_parts, 2 * m + 3 + i)
                    out = bank[:, Q0 + i, :]
                    product(pe, out, halves(V, slice(None), 0), halves(pT, slice(None), slice(i * 512, i * 512 + 512)), True, False)
                    out2 = out.rearrange("p (h s) -> p h s", h=2)[:, :, P:S]
                    x = halves(pT, slice(None), slice(1024 + i * 256, 1024 + i * 256 + 256))
                    x = tuple(a.rearrange("p (h s) -> p h s", h=2) for a in x)
                    mm = product(pe, out2, halves(V, slice(None), 1), x, False, True)
                    mm.then_inc(o_done, 1)

            def step(n, b, g, g_rows):
                scores(n - 1)
                project(n, b, g)
                turn(n - 1)
                if not isinstance(n, int) or n >= 2:
                    rows(n - 2, g_rows)
                values(n - 1)

            pe.wait_ge(consts_in, 64)
            pe.wait_ge(xt_in[0], 32)
            project(0, 0, 0)
            pe.wait_ge(xt_in[1], 32)
            step(1, 1, 0, 0)
            pe.wait_ge(xt_in[2], 32 * (B - 2))
            step(2, 2, 0, 0)
            with pe.Fori(3, B) as b:
                step(b, b, 0, 0)
            with pe.Fori(1, G) as g:
                step(g * B, 0, g, g - 1)
                step(g * B + 1, 1, g, g - 1)
                with pe.Fori(2, B) as b:
                    step(g * B + b, b, g, g)
            scores(STEPS - 1)
            turn(STEPS - 1)
            rows(STEPS - 2, G - 1)
            values(STEPS - 1, last=True)
            rows(STEPS - 1, G - 1)

        @block.scalar
        def _(act):
            def split(g, parts, before, loads):
                if before is not None:
                    act.wait_ge(*before)
                act.wait_ge(raw_in, loads)
                for dst, a, z in parts:
                    ins = act.activation(dst[0][:].rearrange("p a b -> p (a b)"), raw[:, a:z], ACT.Copy)
                    if len(parts) == 1 or a > 0:
                        ins.then_inc(w_hi, 1)

            def split_qkv(g, first=False):
                split(g, kv_parts, None if first else (q_done, 2 * B * g), 32 * g + 16)
                split(g, ((Wq, KV, KV + QO),), None, 32 * g + 16)

            def split_wo(g, first=False):
                split(g, ((Wo, 0, QO),), None if first else (y_done, 2 * B * g), 32 * g + 32)

            def outputs(m):
                for i in range(2):
                    act.wait_ge(o_done, 2 * m + 1 + i)
                    if i == 0 and not (isinstance(m, int) and m == 0):
                        act.wait_ge(y_done, 2 * m)
                    act.activation(o[0][:, 2 * i:2 * i + 2, :], bank[:, Q0 + i, :].rearrange("p (h s) -> p h s", h=2),
                                   ACT.Copy).then_inc(o_hi, 1)

            def softmax(m):
                act.wait_ge(v_turned, m + 1)
                if not (isinstance(m, int) and m == 0):
                    act.wait_ge(o_done, 2 * m)
                act.activation(V[0][:], bank[:, KVB, 0:S].rearrange("p (t d) -> p t d", t=TT), ACT.Copy).then_inc(v_hi, 1)
                for j in range(2 * HG):
                    act.wait_ge(masked, 8 * m + j + 1)
                    h = j % HG
                    t = p[:, h, 2 * P:3 * P] if j < HG else p[:, h, 0:2 * P]
                    act.activation(t, t, ACT.Exp, bias=nmax[:, j:j + 1], scale=-1.0,
                                   accum_out=rsum[:, j:j + 1]).then_inc(exp_done, 1)

            def projected(n):
                act.wait_ge(kv_done, n + 1)
                act.activation(vT[:], bank[:, KVB, S:2 * S], ACT.Copy).then_inc(vT_copied, 1)

            def keys(n):
                act.wait_ge(k_rot, n + 1)
                act.activation(k[0][:], k32[:], ACT.Copy).then_inc(k_hi, 1)

            def queries(n, i):
                act.wait_ge(q_rot, 2 * n + 1 + i)
                act.activation(q[0][:, 2 * i:2 * i + 2, :], q32[:, 2 * i:2 * i + 2, :], ACT.Copy).then_inc(q_hi, 1)

            def turned(m):
                for i in range(3):
                    act.wait_ge(p_turned, 3 * m + 1 + i)
                    if i == 0 and not (isinstance(m, int) and m == 0):
                        act.wait_ge(o_done, 2 * m)
                    act.activation(pT[0][:, i * D:(i + 1) * D], bank[:, S0 + i, :], ACT.Copy).then_inc(pT_hi, 1)

            def step(n):
                if not isinstance(n, int) or n >= 2:
                    outputs(n - 2)
                softmax(n - 1)
                projected(n)
                keys(n)
                queries(n, 0)
                turned(n - 1)
                queries(n, 1)

            split_qkv(0, first=True)
            projected(0), keys(0), queries(0, 0), queries(0, 1)
            step(1)
            split_wo(0, first=True)
            step(2)
            with act.Fori(3, B) as b:
                step(b)
            with act.Fori(1, G) as g:
                split_qkv(g)
                step(g * B)
                step(g * B + 1)
                split_wo(g)
                with act.Fori(2, B) as b:
                    step(g * B + b)
            outputs(STEPS - 2)
            softmax(STEPS - 1)
            turned(STEPS - 1)
            outputs(STEPS - 1)

        @block.vector
        def _(dve):
            def split(g, parts, hi):
                dve.wait_ge(w_hi, hi)
                for dst, a, z in parts:
                    ins = dve.tensor_tensor(dst[1][:].rearrange("p a b -> p (a b)"), raw[:, a:z],
                                            dst[0][:].rearrange("p a b -> p (a b)").bitcast(F32), ALU.subtract)
                    if len(parts) == 1 or a > 0:
                        ins.then_inc(w_lo, 1)

            def split_qkv(g):
                split(g, kv_parts, 3 * g + 1)
                split(g, ((Wq, KV, KV + QO),), 3 * g + 2)

            def split_wo(g):
                split(g, ((Wo, 0, QO),), 3 * g + 3)

            def outputs(m, i):
                dve.wait_ge(o_hi, 2 * m + 1 + i)
                dst = o[1][:, 2 * i:2 * i + 2, :]
                dve.tensor_tensor(dst, bank[:, Q0 + i, :].rearrange("p (h s) -> p h s", h=2),
                                  o[0][:, 2 * i:2 * i + 2, :].bitcast(F32), ALU.subtract).then_inc(o_lo, 1)

            def scored(m, outputs_of=None):
                if outputs_of is not None:
                    outputs(outputs_of, 0)
                if not (isinstance(m, int) and m == 0):
                    dve.wait_ge(p_turned, 3 * m)
                dve.wait_ge(s_done, 3 * m + 1)
                dve.wait_ge(v_hi, m + 1)
                dve.tensor_tensor(V[1][:], bank[:, KVB, 0:S].rearrange("p (t d) -> p t d", t=TT),
                                  V[0][:].bitcast(F32), ALU.subtract).then_inc(v_lo, 1)
                for j in range(2 * HG):
                    h = j % HG
                    if j == HG:
                        dve.wait_ge(s_done, 3 * m + 3)
                        if outputs_of is not None:
                            outputs(outputs_of, 1)
                    if j < HG:
                        t, src, msk = p[:, h, 2 * P:3 * P], bank[:, SQ0, h * P:(h + 1) * P], mask[:, P:S]
                    else:
                        t, src, msk = p[:, h, 0:2 * P], bank[:, S0 + h // 2, h % 2 * S:(h % 2 + 1) * S], mask[:]
                    dve.tensor_tensor_reduce(t, src, msk, -SCALE, BIG, ALU.add, ALU.min,
                                             nmax[:, j:j + 1]).then_inc(masked, 1)

            def normalised(m):
                for half in range(2):
                    c = slice(half * HG, half * HG + HG)
                    dve.wait_ge(exp_done, 8 * m + 4 * half + 4)
                    dve.reciprocal(rinv[:, c], rsum[:, c]).then_inc(rinv_done, 1)
                    dve.wait_ge(rinv_done, 2 * m + half + 1)
                    for h in range(HG):
                        t = p[:, h, 0:2 * P] if half else p[:, h, 2 * P:3 * P]
                        dve.tensor_scalar(t, t, rinv[:, half * HG + h:half * HG + h + 1], None, ALU.mult).then_inc(p_ready, 1)

            def rotate(out, tmp_t, src, heads):
                c = cos[:].unsqueeze(1).to_broadcast([P, heads, S])
                s_lo = sin[0:64].unsqueeze(1).to_broadcast([64, heads, S])
                s_hi = sin[64:128].unsqueeze(1).to_broadcast([64, heads, S])
                dve.tensor_tensor(out, src, c, ALU.mult)
                dve.tensor_tensor(tmp_t[0:64], src[64:128], s_lo, ALU.mult)
                return dve.tensor_tensor(tmp_t[64:128], src[0:64], s_hi, ALU.mult)

            def keys(n):
                dve.wait_ge(vT_copied, n + 1)
                if not isinstance(n, int) or n >= 1:
                    dve.wait_ge(s_done, 3 * n)
                    dve.wait_ge(k_lo, n)
                rotate(k32[:].unsqueeze(1), tmp[:, HG:HG + 1, :], bank[:, KVB, 0:S].unsqueeze(1), 1).then_inc(k_parts, 1)

            def queries(n, i):
                dve.wait_ge(q_done, 2 * n + 1 + i)
                if not isinstance(n, int) or n >= 1:
                    dve.wait_ge(q_lo, 2 * n)
                hs = slice(2 * i, 2 * i + 2)
                rotate(q32[:, hs, :], tmp[:, hs, :], bank[:, Q0 + i, :].rearrange("p (h s) -> p h s", h=2), 2)\
                    .then_inc(q_parts, 1)

            def turned(m):
                for i in range(3):
                    dve.wait_ge(pT_hi, 3 * m + 1 + i)
                    c = slice(i * D, (i + 1) * D)
                    dve.tensor_tensor(pT[1][:, c], bank[:, S0 + i, :], pT[0][:, c].bitcast(F32), ALU.subtract).then_inc(pT_lo, 1)

            def accumulate(m, b):
                for tt in range(TT):
                    dve.wait_ge(y_done, 2 * m + 1 + tt)
                    y = Y[:, TT * b + tt, :]
                    dve.tensor_tensor(y, bank[:, Y0 + tt, :], y, ALU.add).then_inc(y_added, 1)

            def step(n, b_rows):
                scored(n - 1, None if isinstance(n, int) and n < 2 else n - 2)
                keys(n)
                normalised(n - 1)
                queries(n, 0)
                queries(n, 1)
                turned(n - 1)
                if not isinstance(n, int) or n >= 2:
                    accumulate(n - 2, b_rows)

            split_qkv(0)
            dve.wait_ge(consts_in, 64)
            keys(0), queries(0, 0), queries(0, 1)
            step(1, None)
            split_wo(0)
            dve.wait_ge(y_in, 16)
            with dve.Fori(2, B) as b:
                step(b, b - 2)
            with dve.Fori(1, G) as g:
                split_qkv(g)
                step(g * B, B - 2)
                step(g * B + 1, B - 1)
                split_wo(g)
                with dve.Fori(2, B) as b:
                    step(g * B + b, b - 2)
            scored(STEPS - 1, STEPS - 2)
            normalised(STEPS - 1)
            turned(STEPS - 1)
            accumulate(STEPS - 2, B - 2)
            outputs(STEPS - 1, 0)
            outputs(STEPS - 1, 1)
            accumulate(STEPS - 1, B - 1)

        @block.gpsimd
        def _(pool):
            def rotated(n, hi, lo, parts, at, x32, x, t, count, i):
                pool.wait_ge(parts, count * n + 1 + i)
                pool.tensor_tensor(x32, x32, t, ALU.add).then_inc(at, 1)

            def step(n):
                pool.wait_ge(k_parts, n + 1)
                pool.tensor_tensor(k32[:], k32[:], tmp[:, HG, :], ALU.add).then_inc(k_rot, 1)
                pool.wait_ge(k_hi, n + 1)
                pool.tensor_tensor(k[1][:], k32[:], k[0][:].bitcast(F32), ALU.subtract).then_inc(k_lo, 1)
                for i in range(2):
                    hs = slice(2 * i, 2 * i + 2)
                    pool.wait_ge(q_parts, 2 * n + 1 + i)
                    pool.tensor_tensor(q32[:, hs, :], q32[:, hs, :], tmp[:, hs, :], ALU.add).then_inc(q_rot, 1)
                    pool.wait_ge(q_hi, 2 * n + 1 + i)
                    pool.tensor_tensor(q[1][:, hs, :], q32[:, hs, :], q[0][:, hs, :].bitcast(F32), ALU.subtract).then_inc(q_lo, 1)

            with pool.Fori(0, STEPS) as n:
                step(n)


def ffn1(nc, w_ffn, b2_row, ident_t, out, XT, Y):
    G, FT, C = 8, 2, 4
    CT = NT // C
    CB = B // C
    STEPS = G * C
    W1N, W2N = KT * FT * P, FT * D
    with ExitStack() as ctx:
        def sb(name, shape, dt=F32):
            return ctx.enter_context(nc.sbuf_tensor("f1_" + name, shape, dt))

        def sem(name):
            return ctx.enter_context(nc.semaphore("f1_" + name))

        def pair(name, shape):
            return sb(name + "_hi", shape, F32R), sb(name + "_lo", shape, F32R)

        raw1, raw2 = sb("raw1", [P, W1N + FT]), sb("raw2", [P, W2N])
        W1, W2, b1 = pair("W1", [P, KT, FT * P]), pair("W2", [P, FT, D]), sb("b1", [P, FT])
        h32, h = sb("h32", [P, FT, D]), pair("h", [P, FT, D])
        b2, ident = sb("b2", [P, D]), sb("ident", [P, P])
        stats, mv = sb("stats", [P, CT, 6]), sb("mv", [P, CT, 2])
        veps, rstd, mhalf = sb("veps", [P, CT]), sb("rstd", [P, CT]), sb("mhalf", [P, CT])
        bank = ctx.enter_context(nc.psum_tensor("f1_bank", [P, 8, D], F32))
        H0, Y0, X0 = 0, 2, 6

        consts_in, raw1_in, raw2_in = sem("consts_in"), sem("raw1_in"), sem("raw2_in")
        mhalf_set, b1_set, w1_hi, w1_lo, w2_hi, w2_lo = sem("mhalf_set"), sem("b1_set"), sem("w1_hi"), sem("w1_lo"), sem("w2_hi"), sem("w2_lo")
        stats_done, aggr_done, veps_done, rstd_done, normed = (
            sem("stats_done"), sem("aggr_done"), sem("veps_done"), sem("rstd_done"), sem("normed"))
        x_turned, x_hi, x_lo, b2_added = sem("x_turned"), sem("x_hi"), sem("x_lo"), sem("b2_added")
        h_done, gelu_done, h_hi, h_lo = sem("h_done"), sem("gelu_done"), sem("h_hi"), sem("h_lo")
        y_done, y_added, stored = sem("y_done"), sem("y_added"), sem("stored")

        block = ctx.enter_context(nc.Block())

        @block.sync
        def _(sp):
            sp.dma_start(raw1[:], w_ffn[:, 0, 0:W1N + FT]).then_inc(raw1_in, 16)
            sp.dma_start(ident[:], ident_t).then_inc(consts_in, 16)
            sp.dma_start(b2[:], b2_row.partition_broadcast(P)).then_inc(consts_in, 16)
            sp.dma_start(raw2[:], w_ffn[:, 0, W1N + FT:]).then_inc(raw2_in, 16)
            with sp.Fori(1, G) as g:
                sp.wait_ge(w1_lo, g)
                sp.wait_ge(b1_set, g)
                sp.dma_start(raw1[:], w_ffn[:, g, 0:W1N + FT]).then_inc(raw1_in, 16)
                sp.wait_ge(w2_lo, g)
                sp.dma_start(raw2[:], w_ffn[:, g, W1N + FT:]).then_inc(raw2_in, 16)
            for i in range(NT):
                sp.wait_ge(normed, NT + i + 1)
                sp.dma_start(out[:, i, :], Y[:, i, :]).then_inc(stored, 16)
            sp.wait_ge(stored, 16 * NT)

        @block.tensor
        def _(pe):
            chunks = tuple(t[:].rearrange("p (c b) k t -> p c b k t", b=CB) for t in XT)

            def turn(c):
                for j in range(CT):
                    i = CT * c + j
                    pe.wait_ge(normed, i + 1)
                    if i >= 2:
                        pe.wait_ge(x_lo, i - 1)
                    for kt in range(KT):
                        mm = pe.transpose(bank[:, X0 + i % 2, kt * P:(kt + 1) * P], Y[:, i, kt * P:(kt + 1) * P], ident[:])
                    mm.then_inc(x_turned, 1)

            def hidden(s, c, g):
                pe.wait_ge(w1_lo, g + 1)
                for f in range(FT):
                    if not isinstance(s, int) or s >= 1:
                        pe.wait_ge(gelu_done, FT * s - 1 + f)
                    for kt in range(KT):
                        mm = product(pe, bank[:, H0 + f, :].rearrange("p (b t) -> p b t", b=CB),
                                     halves(W1, slice(None), kt, slice(f * P, (f + 1) * P)),
                                     halves(chunks, slice(None), c, slice(None), kt), kt == 0, kt == KT - 1)
                    mm.then_inc(h_done, 1)

            def rows(s, g):
                pe.wait_ge(w2_lo, g + 1)
                pe.wait_ge(h_lo, FT * s + FT)
                for t in range(CT):
                    if not isinstance(s, int) or s >= 1:
                        pe.wait_ge(y_added, CT * s - 3 + t)
                    for f in range(FT):
                        mm = product(pe, bank[:, Y0 + t, :], halves(h, slice(None), f, slice(t * P, (t + 1) * P)),
                                     halves(W2, slice(None), f), f == 0, f == FT - 1)
                    mm.then_inc(y_done, 1)

            pe.wait_ge(consts_in, 32)
            turn(0)
            for c in range(C):
                pe.wait_ge(x_lo, CT * (c + 1))
                hidden(c, c, 0)
                if c + 1 < C:
                    turn(c + 1)
                if c:
                    rows(c - 1, 0)
            with pe.Fori(1, G) as g:
                for c in range(C):
                    hidden(g * C + c, c, g)
                    rows(g * C + c - 1, g if c else g - 1)
            rows(STEPS - 1, G - 1)

        @block.scalar
        def _(act):
            def split_w1(g):
                act.wait_ge(raw1_in, 16 * g + 16)
                if not (isinstance(g, int) and g == 0):
                    act.wait_ge(h_done, FT * C * g)
                act.activation(W1[0][:].rearrange("p a b -> p (a b)"), raw1[:, 0:W1N], ACT.Copy).then_inc(w1_hi, 1)

            def load_b1(g):
                act.activation(b1[:], raw1[:, W1N:W1N + FT], ACT.Copy).then_inc(b1_set, 1)

            def split_w2(g):
                act.wait_ge(raw2_in, 16 * g + 16)
                if not (isinstance(g, int) and g == 0):
                    act.wait_ge(y_done, CT * C * g)
                act.activation(W2[0][:].rearrange("p a b -> p (a b)"), raw2[:], ACT.Copy).then_inc(w2_hi, 1)

            def turned(c):
                for j in range(CT):
                    i = CT * c + j
                    act.wait_ge(x_turned, i + 1)
                    act.activation(XT[0][:, i // TT, :, i % TT * P:(i % TT + 1) * P],
                                   bank[:, X0 + i % 2, :].rearrange("p (k t) -> p k t", k=KT), ACT.Copy).then_inc(x_hi, 1)

            def activate(s, g):
                for f in range(FT):
                    act.wait_ge(h_done, FT * s + f + 1)
                    act.wait_ge(b1_set, g + 1)
                    if f == 0 and not (isinstance(s, int) and s == 0):
                        act.wait_ge(h_lo, FT * s)
                    act.activation(h32[:, f, :], bank[:, H0 + f, :], ACT.Gelu_apprx_tanh, bias=b1[:, f:f + 1]).then_inc(gelu_done, 1)

            def hidden(s):
                act.wait_ge(gelu_done, FT * s + FT)
                if not (isinstance(s, int) and s == 0):
                    act.wait_ge(y_done, CT * s)
                for f in range(FT):
                    act.activation(h[0][:, f, :], h32[:, f, :], ACT.Copy).then_inc(h_hi, 1)

            def group(g, more):
                for c in range(C):
                    if c == C - 1 and more:
                        split_w1(g + 1)
                    activate(g * C + c, g)
                    if isinstance(g, int) and g == 0 and c + 1 < C:
                        turned(c + 1)
                    hidden(g * C + c)
                    if c == 0:
                        split_w2(g)
                if more:
                    load_b1(g + 1)

            split_w1(0)
            load_b1(0)
            turned(0)
            group(0, True)
            with act.Fori(1, G - 1) as g:
                group(g, True)
            group(G - 1, False)

        @block.vector
        def _(dve):
            def normalise(c, done):
                for j in range(CT):
                    dve.bn_stats(stats[:, j, :], Y[:, CT * c + j, :]).then_inc(stats_done, 1)
                for j in range(CT):
                    dve.wait_ge(stats_done, CT * done + j + 1)
                    dve.bn_aggr(mv[:, j, :], stats[:, j, :]).then_inc(aggr_done, 1)
                dve.wait_ge(aggr_done, CT * done + CT)
                dve.tensor_scalar(veps[:], mv[:, :, 1], EPS, None, ALU.add).then_inc(veps_done, 1)
                dve.wait_ge(rstd_done, done + 1)
                for j in range(CT):
                    y = Y[:, CT * c + j, :]
                    dve.tensor_scalar(y, y, mv[:, j, 0:1], rstd[:, j:j + 1], ALU.subtract, ALU.mult).then_inc(normed, 1)

            def turned(c):
                for j in range(CT):
                    i = CT * c + j
                    dve.wait_ge(x_hi, i + 1)
                    xs = (slice(None), i // TT, slice(None), slice(i % TT * P, (i % TT + 1) * P))
                    dve.tensor_tensor(XT[1][xs], bank[:, X0 + i % 2, :].rearrange("p (k t) -> p k t", k=KT),
                                      XT[0][xs].bitcast(F32), ALU.subtract).then_inc(x_lo, 1)

            def hidden(s):
                for f in range(FT):
                    dve.wait_ge(h_hi, FT * s + f + 1)
                    dve.tensor_tensor(h[1][:, f, :], h32[:, f, :], h[0][:, f, :].bitcast(F32), ALU.subtract).then_inc(h_lo, 1)

            def accumulate(s, c):
                for t in range(CT):
                    dve.wait_ge(y_done, CT * s + t + 1)
                    y = Y[:, CT * c + t, :]
                    dve.tensor_tensor(y, bank[:, Y0 + t, :], y, ALU.add).then_inc(y_added, 1)

            normalise(0, 0)
            turned(0)
            for c in range(C):
                if c + 1 < C:
                    normalise(c + 1, c + 1)
                    turned(c + 1)
                hidden(c)
                if c:
                    dve.wait_ge(b2_added, CT * c)
                    accumulate(c - 1, c - 1)
            dve.wait_ge(b2_added, NT)
            with dve.Fori(1, G - 1) as g:
                for c in range(C):
                    hidden(g * C + c)
                    accumulate(g * C + c - 1, (c - 1) % C)
            hidden((G - 1) * C)
            accumulate((G - 1) * C - 1, C - 1)
            for c in range(1, C + 1):
                if c < C:
                    hidden((G - 1) * C + c)
                accumulate((G - 1) * C + c - 1, c - 1)
                dve.wait_ge(y_added, CT * ((G - 1) * C + c))
                normalise(c - 1, C + c - 1)

        @block.gpsimd
        def _(pool):
            def split(pair_w, raw, size, hi, lo, g):
                pool.wait_ge(hi, g + 1)
                pool.tensor_tensor(pair_w[1][:].rearrange("p a b -> p (a b)"), raw[:, 0:size],
                                   pair_w[0][:].rearrange("p a b -> p (a b)").bitcast(F32), ALU.subtract).then_inc(lo, 1)

            def rescale(n):
                pool.wait_ge(veps_done, n + 1)
                pool.tensor_tensor(rstd[:], veps[:], mhalf[:], ALU.pow).then_inc(rstd_done, 1)

            pool.memset(mhalf[:], -0.5).then_inc(mhalf_set, 1)
            pool.wait_ge(mhalf_set, 1)
            rescale(0)
            split(W1, raw1, W1N, w1_hi, w1_lo, 0)
            pool.wait_ge(consts_in, 32)
            for n in range(C):
                if n + 1 < C:
                    rescale(n + 1)
                if n == 0:
                    split(W2, raw2, W2N, w2_hi, w2_lo, 0)
                for j in range(CT):
                    i = CT * n + j
                    pool.wait_ge(x_turned, i + 1)
                    pool.tensor_tensor(Y[:, i, :], Y[:, i, :], b2[:], ALU.add).then_inc(b2_added, 1)
            with pool.Fori(1, G) as g:
                split(W1, raw1, W1N, w1_hi, w1_lo, g)
                split(W2, raw2, W2N, w2_hi, w2_lo, g)
            for n in range(C):
                rescale(C + n)


def two_layers(nc, ins, out):
    x2 = nc.dram_tensor("x2", [P, B, TT, D], F32, kind="Internal").ap()
    x2T_hi = nc.dram_tensor("x2T_hi", [P, B, KT, S], F32, kind="Internal").ap()
    x2T_lo = nc.dram_tensor("x2T_lo", [P, B, KT, S], F32, kind="Internal").ap()
    layer0(nc, ins["xT"], ins["x"], ins["w_qkv0"], ins["w_o0"], ins["w_base"], ins["w_lr"], ins["w_lb"], ins["b_base"],
           ins["b_router"], ins["cos0"], ins["sin0"], ins["mask"], ins["ident"], ins["inv_k"], x2, x2T_hi, x2T_lo)
    with ExitStack() as ctx:
        XT = tuple(ctx.enter_context(nc.sbuf_tensor("XT" + n, [P, B, KT, S], F32R)) for n in ("_hi", "_lo"))
        Y = ctx.enter_context(nc.sbuf_tensor("Y", [P, NT, D], F32))
        attention1(nc, x2.rearrange("p b t d -> p (b t) d"), x2T_hi, x2T_lo, ins["w_attn1"], ins["cos1"], ins["sin1"],
                   ins["mask"], ins["ident"], XT, Y)
        ffn1(nc, ins["w_ffn1"], ins["b2"], ins["ident"], out.rearrange("b (t p) d -> p (b t) d", p=P), XT, Y)


def kernel(**inputs):
    import concourse.bacc as bacc
    from concourse.bass_utils import run_bass_kernel_spmd

    a = {name: np.asarray(v) for name, v in inputs.items()}

    def by_contraction(w):
        return w.reshape(KT, P, -1).transpose(1, 0, 2)

    def by_group(w):
        return w.reshape(KT, P, 8, -1).transpose(1, 2, 0, 3).reshape(P, 8, -1)

    def by_token_tile(t):
        return t.reshape(TT, P, -1).transpose(1, 0, 2)

    even_odd = np.concatenate([np.arange(0, 16, 2), np.arange(1, 16, 2)])

    def split_pairs(w):
        return w.reshape(D, -1, 16)[:, :, even_odd].reshape(D, -1)

    pos = np.arange(S, dtype=np.float32)[:, None]
    freq0 = 1.0 / np.float32(10000.0) ** (np.arange(0, 16, 2, dtype=np.float32) / np.float32(16))
    angle0 = pos * freq0.astype(np.float32)
    inv = 1.0 / 500000.0 ** (np.arange(0, 128, 2, dtype=np.float64) / 128)
    wavelen = 2.0 * np.pi / inv
    smooth = (1024 / wavelen - 1.0) / (4.0 - 1.0)
    scaled = np.where(wavelen > 1024 / 1.0, inv / 8.0, inv)
    mid = (wavelen <= 1024 / 1.0) & (wavelen >= 1024 / 4.0)
    scaled = np.where(mid, (1 - smooth) * inv / 8.0 + smooth * inv, scaled).astype(np.float32)
    angle1 = np.concatenate([pos * scaled[None, :]] * 2, axis=-1)
    sin1 = np.sin(angle1).T.copy()
    sin1[:P // 2] *= -1
    mask = np.zeros((P, S), np.float32)
    mask[:, P:] = np.where(np.arange(P)[:, None] >= np.arange(P)[None], 0, -1e30)

    x, wb = a["L0_attn_x"], a["L0_ffn_W_base"]
    lora_a = a["L0_ffn_lora_A"].transpose(1, 0, 2).reshape(D, -1)
    arrays = {
        "xT": x.reshape(B, S, KT, P).transpose(3, 0, 2, 1),
        "x": x.reshape(B, TT, P, D).transpose(2, 0, 1, 3),
        "w_qkv0": by_contraction(np.concatenate([split_pairs(a["L0_attn_Wq"]), split_pairs(a["L0_attn_Wk"]), a["L0_attn_Wv"]], 1)),
        "w_o0": by_contraction(a["L0_attn_Wo"]),
        "w_base": by_contraction(wb.T),
        "w_lr": by_contraction(np.concatenate([lora_a, a["L0_ffn_W_router"].T], 1)),
        "w_lb": a["L0_ffn_lora_B"].reshape(P, D),
        "b_base": a["L0_ffn_b_base"],
        "b_router": a["L0_ffn_b_router"],
        "cos0": by_token_tile(np.cos(np.concatenate([angle0, angle0], 1))),
        "sin0": by_token_tile(np.concatenate([-np.sin(angle0), np.sin(angle0)], 1)),
        "cos1": np.cos(angle1).T,
        "sin1": sin1,
        "mask": mask,
        "ident": np.eye(P),
        "inv_k": np.broadcast_to(1.0 / np.arange(1, 9), (P, 8)),
        "w_attn1": np.concatenate([by_group(a["L1_attn_wk"]), by_group(a["L1_attn_wv"]), by_group(a["L1_attn_wq"]),
                                   a["L1_attn_wo"].reshape(8, 4, P, D).transpose(2, 0, 1, 3).reshape(P, 8, -1)], 2),
        "w_ffn1": np.concatenate([by_group(a["L1_ffn_W1"]), a["L1_ffn_fc1_bias"].reshape(8, 2, P).transpose(2, 0, 1),
                                  a["L1_ffn_W2"].reshape(8, 2, P, D).transpose(2, 0, 1, 3).reshape(P, 8, -1)], 2),
        "b2": a["L1_ffn_fc2_bias"],
    }
    arrays = {name: np.ascontiguousarray(v, dtype=np.float32) for name, v in arrays.items()}
    nc = bacc.Bacc("TRN2", target_bir_lowering=False, num_devices=1)
    ins = {name: nc.dram_tensor(name, v.shape, F32, kind="ExternalInput").ap() for name, v in arrays.items()}
    out = nc.dram_tensor("out", (B, S, D), F32, kind="ExternalOutput").ap()
    two_layers(nc, ins, out)
    result = run_bass_kernel_spmd(nc, [arrays], core_ids=[0])
    return result.results[0]["out"]
```

```python
import numpy as np
import concourse.bass as bass
from concourse import mybir
from contextlib import ExitStack

F32 = mybir.dt.float32
F32R = mybir.dt.float32r
ALU = mybir.AluOpType
ACT = mybir.ActivationFunctionType
AX = mybir.AxisListType

P = 128
D = 512
KT = D // P
B, S = 8, 256
TT = S // P
NT = B * TT
BIG = 3.0e38
EPS = 1e-5


def product(pe, out, w, x, first=True, last=True):
    pe.matmul(out, w[0], x[0], start=first, stop=False)
    pe.matmul(out, w[0], x[1], start=False, stop=False)
    return pe.matmul(out, w[1], x[0], start=False, stop=last)


def halves(pair, *index):
    return tuple(t[index] for t in pair)


def layer0(nc, xT_in, x_in_t, w_qkv, w_o, w_base, w_lr, w_lb, b_base_row, b_router_row, cos_t, sin_t, mask_t, ident_t,
           inv_k, x2, x2T_hi, x2T_lo, stage, mask, ident, later, early, rows, last, x2T_stored):
    H, G, HD, E, R = 32, 8, 16, 8, 16
    HP, NP = HD // 2, H // 2
    QW, KW = H * HD, G * HD
    SCALE = 0.25
    VC = 32
    with ExitStack() as ctx:
        def sb(name, shape, dt=F32):
            return ctx.enter_context(nc.sbuf_tensor("l0_" + name, shape, dt))

        def sem(name):
            return ctx.enter_context(nc.semaphore("l0_" + name))

        def pair(name, shape):
            return sb(name + "_hi", shape, F32R), sb(name + "_lo", shape, F32R)

        raw = stage[:].bitcast(F32).rearrange("p (k c) -> p k c", k=KT)
        AFTER = 2 * KT * P
        x2T = tuple(stage[:, AFTER + i * KT * S:AFTER + (i + 1) * KT * S].rearrange("p (k t) -> p k t", k=KT) for i in range(2))
        Wqkv, Wo, Wb, Lb = (pair("Wqkv", [P, KT, QW + 2 * KW]), pair("Wo", [P, KT, D]), pair("Wb", [P, KT, D]), pair("Lb", [P, D]))
        Lr = sb("Lr", [P, KT, P + E])
        b_base, b_router, invk = sb("b_base", [P, D]), sb("b_router", [P, E]), sb("invk", [P, E])
        cos, sin = sb("cos", [P, TT, HD]), sb("sin", [P, TT, HD])
        ident_r, mhalf = sb("ident_r", [P, P], F32R), sb("mhalf", [P, 1])
        xT32, xT, X = rows[:, 0:KT * S].rearrange("p (k t) -> p k t", k=KT), pair("xT", [P, KT, S]), sb("X", [P, TT, D])
        rq, tq = (rows[:, KT * S + i * H * HD:KT * S + (i + 1) * H * HD].rearrange("p (h d) -> p h d", h=H) for i in range(2))
        rk, tk, v32 = sb("rk", [P, TT, G, HD]), sb("tk", [P, TT, G, HD]), sb("v32", [P, TT, G, HD])
        Qs = tuple(sb(f"Qs{t}", [P, H, 2, 2, HD], F32R) for t in range(TT))
        Ks = tuple(early[:, t].rearrange("p k t -> p (k t)").rearrange("p (g a c d) -> p g a c d", g=G, a=4, c=2) for t in range(TT))
        QT = sb("QT", [P, NP, S], F32R)
        KZ = sb("KZ", [P, G, 2, S], F32R)
        V = sb("V", [P, TT, G, VC])
        gate = sb("gate", [P, 3])
        p, nmax = sb("p", [P, 2, 2, 3 * P]), sb("nmax", [P, 2, 4])
        pT = sb("pT", [P, 2, 6 * P])
        ot, rinv, Oat = sb("ot", [P, S]), sb("rinv", [P, TT, 4]), sb("Oat", [P, TT, H, HD])
        OT, x1T32, x1T = pair("OT", [P, KT, S]), sb("x1T32", [P, KT, S]), pair("x1T", [P, KT, S])
        stats, mv = sb("stats", [P, TT, 6]), sb("mv", [P, TT, 2])
        veps, rstd = sb("veps", [P, TT]), sb("rstd", [P, TT])
        z, c0, c1, c2, tau = sb("z", [P, TT, E]), sb("c0", [P, TT, 12]), sb("c1", [P, TT, 12]), sb("c2", [P, TT, 12]), sb("tau", [P, TT])
        c3, hw, hwT = sb("c3", [P, TT, E]), sb("hw", [P, TT, P]), pair("hwT", [P, S])
        bank = ctx.enter_context(nc.psum_tensor("l0_bank", [P, 8, D], F32))
        OB, F0, F1, F2 = 4, 5, 6, 7
        QB = {(0, 0): F2, (1, 0): F0, (0, 1): F0, (1, 1): F0, (2, 0): F0, (2, 1): F2, (3, 0): F0, (3, 1): F1}
        KB = {(0, 0): F2, (0, 1): F2, (1, 0): F2, (1, 1): F1}
        QI = {kt: i for i, kt in enumerate(QB)}

        dve_zeroed, consts_in, xt_in, x_in, raw_in, zeroed = (
            sem("dve_zeroed"), sem("consts_in"), sem("xt_in"), sem("x_in"), sem("raw_in"), sem("zeroed"))
        w_hi, w_lo, ident_set, xs_hi, xs_lo, q_done = (
            sem("w_hi"), sem("w_lo"), sem("ident_set"), sem("xs_hi"), sem("xs_lo"), sem("q_done"))
        kv_done, q_parts, k_parts, v_staged, q_rot, k_rot = (
            sem("kv_done"), sem("q_parts"), sem("k_parts"), sem("v_staged"), sem("q_rot"), sem("k_rot"))
        q_hi, q_lo, k_hi, k_lo, q_turned, k_turned = (
            sem("q_hi"), sem("q_lo"), sem("k_hi"), sem("k_lo"), sem("q_turned"), sem("k_turned"))
        qt_done, kz_top, kz_bottom, v_set, s_done, masked = (
            sem("qt_done"), sem("kz_top"), sem("kz_bottom"), sem("v_set"), sem("s_done"), sem("masked"))
        exp_done, p_turned, pT0_done, pT1_done, pv_done, ot_done = (
            sem("exp_done"), sem("p_turned"), sem("pT0_done"), sem("pT1_done"), sem("pv_done"), sem("ot_done"))
        o_turned, rinv_done, o_out, oT_turned, oT_hi, oT_lo = (
            sem("o_turned"), sem("rinv_done"), sem("o_out"), sem("oT_turned"), sem("oT_hi"), sem("oT_lo"))
        r_done, added, stats_done, aggr_done, veps_done, rstd_done = (
            sem("r_done"), sem("added"), sem("stats_done"), sem("aggr_done"), sem("veps_done"), sem("rstd_done"))
        normed, x1_turned, x1_32, x1_hi, x1_lo, b_added = (
            sem("normed"), sem("x1_turned"), sem("x1_32"), sem("x1_hi"), sem("x1_lo"), sem("b_added"))
        lr_done, routing_steps, hw_done, hw_turned, hwT_hi, hwT_lo = (
            sem("lr_done"), sem("routing_steps"), sem("hw_done"), sem("hw_turned"), sem("hwT_hi"), sem("hwT_lo"))
        z_done, x2_turned, x2_hi, x2_lo, x2_stored = (
            sem("z_done"), sem("x2_turned"), sem("x2_hi"), sem("x2_lo"), sem("x2_stored"))
        later_in, last_in, tables_in, qkv_in = sem("later_in"), sem("last_in"), sem("tables_in"), [sem(f"qkv_in{kt}") for kt in range(KT)]
        gate_passed, variance_gate, sorting_gate = sem("gate_passed"), sem("variance_gate"), sem("sorting_gate")
        block = ctx.enter_context(nc.Block())

        def wait(eng, semaphore, value, total=None):
            if isinstance(value, int):
                if total is not None:
                    value = min(value, total)
                if value <= 0:
                    return
            eng.wait_ge(semaphore, value)

        def tok(t):
            return slice(t * P, (t + 1) * P)

        def kt_view(ap):
            return ap.rearrange("p (k t) -> p k t", k=KT)

        def stackers(eng):
            def stack_queries(n, t):
                wait(eng, q_parts, 2 * n + 1 + t)
                wait(eng, q_turned, 8 * n)
                eng.tensor_tensor(Qs[t][:, :, 0], rq[:].unsqueeze(2).to_broadcast([P, H, 2, HD]), tq[:].unsqueeze(2).to_broadcast([P, H, 2, HD]),
                                   ALU.add).then_inc(q_hi, 1)
                wait(eng, q_hi, 2 * n + 1 + t)
                eng.tensor_tensor(rq[:], rq[:], tq[:], ALU.add).then_inc(q_rot, 1)
                wait(eng, q_rot, 2 * n + 1 + t)
                eng.tensor_tensor(Qs[t][:, :, 1], rq[:].unsqueeze(2).to_broadcast([P, H, 2, HD]), Qs[t][:, :, 0].bitcast(F32),
                                   ALU.subtract).then_inc(q_lo, 1)

            def stack_keys(n):
                wait(eng, k_parts, n + 1)
                wait(eng, k_turned, 4 * n)
                for t in range(TT):
                    eng.tensor_tensor(Ks[t][:, :, :, 0], rk[:, t].unsqueeze(2).to_broadcast([P, G, 4, HD]),
                                       tk[:, t].unsqueeze(2).to_broadcast([P, G, 4, HD]), ALU.add).then_inc(k_hi, 1)
                wait(eng, k_hi, 2 * n + 2)
                eng.tensor_tensor(rk[:], rk[:], tk[:], ALU.add).then_inc(k_rot, 1)
                wait(eng, k_rot, n + 1)
                for t in range(TT):
                    ins = eng.tensor_tensor(Ks[t][:, :, :, 1], rk[:, t].unsqueeze(2).to_broadcast([P, G, 4, HD]),
                                             Ks[t][:, :, :, 0].bitcast(F32), ALU.subtract)
                ins.then_inc(k_lo, 1)

            return stack_queries, stack_keys

        @block.sync
        def _(sp):
            sp.dma_start(xT32[:], xT_in[:, 0]).then_inc(xt_in, 16)
            for kt in range(KT):
                sp.dma_start(raw[:, kt], w_qkv[:, kt]).then_inc(qkv_in[kt], 16)
                if kt == 0:
                    for t, src in ((ident, ident_t), (cos, cos_t), (sin, sin_t)):
                        sp.dma_start(t[:], src).then_inc(consts_in, 16)
            for t, src in ((mask, mask_t), (invk, inv_k), (b_router, b_router_row.partition_broadcast(P)),
                           (b_base, b_base_row.partition_broadcast(P)), (Lr, w_lr)):
                sp.dma_start(t[:], src).then_inc(tables_in, 16)
            sp.dma_start(X[:], x_in_t[:, 0]).then_inc(x_in, 16)
            sp.wait_ge(xs_lo, 1)
            sp.dma_start(xT32[:], xT_in[:, 1]).then_inc(xt_in, 16)
            for i, (src, n) in enumerate(((w_o, D), (w_base, D))):
                sp.wait_ge(w_lo, KT + i)
                sp.dma_start(raw[:, :, 0:n], src).then_inc(raw_in, 16)
            sp.wait_ge(w_lo, KT + 2)
            sp.dma_start(raw[:, 0, 0:D], w_lb).then_inc(raw_in, 16)

            def batch(m, load_x, load_xt):
                if load_xt is not None:
                    sp.wait_ge(xs_lo, load_xt)
                    sp.dma_start(xT32[:], xT_in[:, load_xt]).then_inc(xt_in, 16)
                for t in range(TT):
                    sp.wait_ge(normed, 4 * m + 3 + t)
                    sp.dma_start(x2[:, m, t], X[:, t]).then_inc(x2_stored, 16)
                if load_x is not None:
                    sp.wait_ge(x2_turned, 2 * m + 2)
                    sp.wait_ge(x2_stored, 32 * m + 32)
                    sp.dma_start(X[:], x_in_t[:, load_x]).then_inc(x_in, 16)
                sp.wait_ge(x2_lo, 2 * m + 2)
                sp.dma_start(x2T_hi[:, m], x2T[0].bitcast(F32)).then_inc(x2T_stored, 16)
                sp.dma_start(x2T_lo[:, m], x2T[1].bitcast(F32)).then_inc(x2T_stored, 16)

            sp.wait_ge(xs_lo, 2)
            sp.dma_start(xT32[:], xT_in[:, 2]).then_inc(xt_in, 16)
            sp.wait_ge(w_lo, KT + 3)
            for t, src in later:
                sp.dma_start(t, src).then_inc(later_in, 16)
            sp.wait_ge(later_in, 16 * len(later))
            batch(0, 1, 3)
            with sp.Fori(1, B - 3) as m:
                batch(m, m + 1, m + 3)
            batch(B - 3, B - 2, None)
            sp.wait_ge(k_turned, 4 * B)
            sp.wait_ge(xs_lo, B)
            sp.wait_ge(q_lo, 2 * B)
            sp.wait_ge(x2T_stored, 32)
            for t, src in last:
                sp.dma_start(t, src).then_inc(last_in, 16)
            batch(B - 2, B - 1, None)
            batch(B - 1, None, None)
            sp.wait_ge(last_in, 16 * len(last))
            sp.wait_ge(x2_stored, 32 * B)

        @block.tensor
        def _(pe):
            def queries(n, t, part):
                if part == 0 and t == 0:
                    wait(pe, xs_lo, n + 1)
                    wait(pe, qt_done, 8 * n - 1)
                elif part == 0:
                    wait(pe, k_parts, n + 1)
                    wait(pe, v_staged, n + 1)
                for kt in (2 * part, 2 * part + 1):
                    if isinstance(n, int) and n == 0:
                        wait(pe, w_lo, kt + 1)
                    mm = product(pe, bank[:, (F0, F1)[t], :], halves(xT, slice(None), kt, tok(t)),
                                 halves(Wqkv, slice(None), kt, slice(0, QW)), kt == 0, kt == KT - 1)
                if part == 1:
                    mm.then_inc(q_done, 1)

            def keys_values(n, t):
                if t == 0:
                    wait(pe, kz_top, 4 * n)
                    wait(pe, kz_bottom, 4 * n)
                for kt in range(KT):
                    mm = product(pe, bank[:, F1, t * S:(t + 1) * S], halves(xT, slice(None), kt, tok(t)),
                                 halves(Wqkv, slice(None), kt, slice(QW, QW + 2 * KW)), kt == 0, kt == KT - 1)
                if t == 1:
                    mm.then_inc(kv_done, 1)

            def turn_queries(n, k, t):
                wait(pe, q_lo, 2 * n + 1 + t)
                if (k, t) == (0, 0):
                    wait(pe, added, 4 * n - 7)
                    wait(pe, kz_top, 4 * n - 1)
                    wait(pe, kz_bottom, 4 * n - 1)
                elif (k, t) == (1, 0):
                    wait(pe, added, 4 * n - 6)
                    wait(pe, q_parts, 2 * n + 1)
                elif (k, t) == (0, 1):
                    wait(pe, hwT_lo, n - 1)
                    wait(pe, qt_done, 8 * n + 2)
                elif (k, t) == (2, 1):
                    wait(pe, added, 4 * n - 4)
                    wait(pe, kz_top, 4 * n + 2)
                    wait(pe, kz_bottom, 4 * n + 2)
                elif (k, t) == (3, 0):
                    wait(pe, qt_done, 8 * n + QI[2, 0] + 1)
                elif (k, t) == (3, 1):
                    wait(pe, x2_lo, 2 * n - 3)
                    wait(pe, q_parts, 2 * n + 2)
                else:
                    wait(pe, qt_done, 8 * n + QI[k, t])
                for j in range(4):
                    i = 4 * k + j
                    mm = pe.transpose(bank[:, QB[k, t], tok(j)].bitcast(F32R),
                                      Qs[t][:, 2 * i:2 * i + 2].rearrange("p h a c d -> p (h a c d)"), ident_r[:])
                mm.then_inc(q_turned, 1)

            def turn_keys(n, k, t):
                wait(pe, k_lo, n + 1)
                if (k, t) == (0, 0):
                    wait(pe, qt_done, 8 * n + 1)
                elif (k, t) == (0, 1):
                    wait(pe, x1_hi, 2 * n - 3)
                    wait(pe, kz_top, 4 * n + 1)
                    wait(pe, kz_bottom, 4 * n + 1)
                elif (k, t) == (1, 0):
                    wait(pe, x2_lo, 2 * n - 2)
                    wait(pe, qt_done, 8 * n + QI[2, 1] + 1)
                else:
                    wait(pe, qt_done, 8 * n + 8)
                for j in range(4):
                    g = 4 * k + j
                    mm = pe.transpose(bank[:, KB[k, t], tok(j)].bitcast(F32R), Ks[t][:, g].rearrange("p a c d -> p (a c d)"), ident_r[:])
                mm.then_inc(k_turned, 1)

            def scores(n, i):
                N, st, g = NP * n + i, i % 2, i // 2
                if i % 4 == 0:
                    wait(pe, qt_done, 8 * n + QI[i // 4, 1] + 1)
                if i % 8 == 0:
                    wait(pe, kz_top, 4 * n + 2 * (i // 8) + 2)
                    wait(pe, kz_bottom, 4 * n + 2 * (i // 8) + 2)
                wait(pe, pT0_done, N - 1)
                wait(pe, pT1_done, N - 1)
                pe.matmul(bank[:, 2 * st, :], QT[:, i, P:S], KZ[:, g], start=True, stop=True)
                pe.matmul(bank[:, 2 * st + 1, 0:S], QT[:, i, 0:P], KZ[:, g, :, 0:P], start=True, stop=True).then_inc(s_done, 1)

            def turn(n, i):
                N, st = NP * n + i, i % 2
                wait(pe, exp_done, 4 * N + 4)
                for h in range(2):
                    pe.transpose(bank[:, 2 * st, h * S:h * S + P], p[:, st, h, 2 * P:3 * P], ident[:])
                    mm = pe.transpose(bank[:, 2 * st, h * S + P:(h + 1) * S], p[:, st, h, 0:P], ident[:])
                mm.then_inc(p_turned, 1)
                for h in range(2):
                    mm = pe.transpose(bank[:, 2 * st + 1, h * P:(h + 1) * P], p[:, st, h, P:2 * P], ident[:])
                mm.then_inc(p_turned, 1)

            def weigh(n, i):
                N, st, g = NP * n + i, i % 2, i // 2
                wait(pe, pT0_done, N + 1)
                wait(pe, pT1_done, N + 1)
                if i == 0:
                    wait(pe, v_set, n + 1)
                if i % 2 == 0:
                    wait(pe, o_out, G * n + g)
                for h in range(2):
                    j = 2 * (i % 2) + h
                    pe.matmul(bank[VC * j:VC * (j + 1), OB, 0:S], V[:, 0, g], pT[:, st, h * S:(h + 1) * S], start=True, stop=False)
                for h in range(2):
                    j = 2 * (i % 2) + h
                    mm = pe.matmul(bank[VC * j:VC * (j + 1), OB, P:S], V[:, 1, g], pT[:, st, 4 * P + h * P:4 * P + (h + 1) * P],
                                   start=False, stop=True)
                mm.then_inc(pv_done, 1)

            def turn_group(n, g):
                wait(pe, ot_done, G * n + g + 1)
                for t in range(TT):
                    mm = pe.transpose(bank[:, OB, S + t * P:S + (t + 1) * P], ot[:, tok(t)], ident[:])
                mm.then_inc(o_turned, 1)

            def turn_outputs(m, t):
                wait(pe, o_out, G * m + G)
                if t == 0:
                    wait(pe, x2_lo, 2 * m)
                    wait(pe, kz_top, 4 * m + 7, 4 * B)
                    wait(pe, kz_bottom, 4 * m + 7, 4 * B)
                else:
                    wait(pe, oT_lo, 2 * m + 1)
                o = Oat[:, t].rearrange("p h d -> p (h d)")
                for kt in range(KT):
                    mm = pe.transpose(bank[:, F2, tok(kt)], o[:, tok(kt)], ident[:])
                mm.then_inc(oT_turned, 1)

            def attention_rows(m, t, part):
                if part == 0:
                    wait(pe, oT_lo, 2 * m + 2)
                    wait(pe, w_lo, KT + 1)
                if t == 1 and part == 0:
                    wait(pe, q_parts, 2 * m + 5, 2 * B)
                    wait(pe, qt_done, 8 * m + 15, 8 * B)
                for kt in (2 * part, 2 * part + 1):
                    mm = product(pe, bank[:, (F2, F0)[t], :], halves(OT, slice(None), kt, tok(t)), halves(Wo, slice(None), kt),
                                 kt == 0, kt == KT - 1)
                if part == 1:
                    mm.then_inc(r_done, 1)

            def turn_x1(m, t):
                wait(pe, normed, 4 * m + 1 + t)
                if t == 0:
                    wait(pe, kz_top, 4 * m + 9, 4 * B)
                    wait(pe, kz_bottom, 4 * m + 9, 4 * B)
                else:
                    wait(pe, qt_done, 8 * m + 18, 8 * B)
                for kt in range(KT):
                    mm = pe.transpose(bank[:, (F2, F0)[t], tok(kt)], X[:, t, tok(kt)], ident[:])
                mm.then_inc(x1_turned, 1)

            def lora_down(m):
                wait(pe, x1_32, 2 * m + 2)
                wait(pe, x1_hi, 2 * m + 2)
                for t in range(TT):
                    for kt in range(KT):
                        mm = pe.matmul(bank[:, F0, t * S:t * S + P + E], x1T32[:, kt, tok(t)], Lr[:, kt], start=kt == 0, stop=kt == KT - 1)
                mm.then_inc(lr_done, 1)

            def base(m, t, part):
                if part == 0:
                    wait(pe, w_lo, KT + 2)
                    wait(pe, x1_hi, 2 * m + 2)
                    wait(pe, x1_lo, 2 * m + 1 + t)
                if part == 0:
                    if t == 0:
                        wait(pe, q_parts, 2 * m + 6, 2 * B)
                    wait(pe, kz_top, 4 * m + (8, 10)[t], 4 * B)
                    wait(pe, kz_bottom, 4 * m + (8, 10)[t], 4 * B)
                for kt in (2 * part, 2 * part + 1):
                    mm = product(pe, bank[:, (F1, F2)[t], :], halves(x1T, slice(None), kt, tok(t)), halves(Wb, slice(None), kt), kt == 0, False)

            def turn_weighted(m):
                wait(pe, hw_done, m + 1)
                for t in range(TT):
                    mm = pe.transpose(bank[:, F0, tok(t)], hw[:, t], ident[:])
                mm.then_inc(hw_turned, 1)

            def lora_up(m, t):
                wait(pe, hwT_lo, m + 1)
                wait(pe, w_lo, KT + 3)
                product(pe, bank[:, (F1, F2)[t], :], halves(hwT, slice(None), tok(t)), halves(Lb, slice(None)), False, True).then_inc(z_done, 1)

            def turn_x2(m, t):
                wait(pe, normed, 4 * m + 3 + t)
                if t == 1:
                    wait(pe, qt_done, 8 * m + 22, 8 * B)
                for kt in range(KT):
                    mm = pe.transpose(bank[:, (F1, F2)[t], tok(kt)], X[:, t, tok(kt)], ident[:])
                mm.then_inc(x2_turned, 1)

            def batch(b, heads, tails):
                m, n, first = b - 1, b + 1, isinstance(b, int) and b == 0
                for i in range(NP):
                    turn(b, i)
                    if i == 0:
                        turn_queries(b, 3, 1)
                    if i == 1:
                        if heads:
                            queries(n, 0, 1)
                        turn_keys(b, 1, 1)
                    if i == 3:
                        if heads:
                            keys_values(n, 1)
                    if i == 5:
                        if tails:
                            attention_rows(m, 1, 0)
                    if i == 7:
                        if heads:
                            turn_keys(n, 0, 0)
                    if i == 9:
                        if heads:
                            turn_keys(n, 0, 1)
                    if i == 11:
                        if tails:
                            base(m, 0, 1)
                            turn_weighted(m)
                    if i == 12:
                        if tails:
                            base(m, 1, 1)
                    if i % 2 == 0 and i > 0:
                        turn_group(b, i // 2 - 1)
                    if i == 0 and not first:
                        turn_group(m, G - 1)
                    if i == 0:
                        turn_keys(b, 1, 0)
                        if heads:
                            queries(n, 0, 0)
                    if i == 2:
                        if tails:
                            turn_outputs(m, 1)
                        if heads:
                            keys_values(n, 0)
                    if i == 3:
                        if tails:
                            attention_rows(m, 0, 0)
                    if i == 4:
                        if tails:
                            attention_rows(m, 0, 1)
                    if i == 5:
                        if tails:
                            attention_rows(m, 1, 1)
                    if i == 6:
                        if heads:
                            queries(n, 1, 0)
                    if i == 7:
                        if heads:
                            queries(n, 1, 1)
                            turn_queries(n, 1, 0)
                    if i == 8:
                        if tails:
                            turn_x1(m, 0)
                            turn_x1(m, 1)
                    if i == 9:
                        if tails:
                            lora_down(m)
                    if i == 10:
                        if tails:
                            base(m, 0, 0)
                    if i == 12:
                        if tails:
                            lora_up(m, 0)
                            lora_up(m, 1)
                    if i == 13:
                        if heads:
                            turn_queries(n, 1, 1)
                    if i == 14:
                        if heads:
                            turn_queries(n, 2, 0)
                            turn_queries(n, 2, 1)
                    if i == 15:
                        if tails:
                            turn_x2(m, 0)
                            turn_x2(m, 1)
                        if heads:
                            turn_queries(n, 3, 0)
                    if i + 2 < NP:
                        scores(b, i + 2)
                    elif heads:
                        scores(n, i + 2 - NP)
                    if i == 6:
                        if heads:
                            turn_queries(n, 0, 0)
                    if i == 10:
                        if tails:
                            base(m, 1, 0)
                    if i == 12:
                        if heads:
                            turn_queries(n, 0, 1)
                    weigh(b, i)
                    if i == 0:
                        if tails:
                            turn_outputs(m, 0)

            def prologue(n):
                queries(n, 0, 0)
                queries(n, 0, 1)
                keys_values(n, 0)
                keys_values(n, 1)
                queries(n, 1, 0)
                turn_queries(n, 0, 0)
                turn_keys(n, 0, 0)
                queries(n, 1, 1)
                turn_queries(n, 1, 0)
                turn_keys(n, 0, 1)
                turn_queries(n, 0, 1)
                turn_queries(n, 1, 1)
                turn_queries(n, 2, 0)
                turn_queries(n, 2, 1)
                turn_queries(n, 3, 0)

            def epilogue(m):
                turn_outputs(m, 0)
                turn_outputs(m, 1)
                attention_rows(m, 0, 0)
                attention_rows(m, 0, 1)
                attention_rows(m, 1, 0)
                attention_rows(m, 1, 1)
                turn_x1(m, 0)
                turn_x1(m, 1)
                lora_down(m)
                base(m, 0, 0)
                base(m, 1, 0)
                base(m, 0, 1)
                turn_weighted(m)
                base(m, 1, 1)
                lora_up(m, 0)
                lora_up(m, 1)
                turn_x2(m, 0)
                turn_x2(m, 1)

            wait(pe, consts_in, 16 * 3)
            wait(pe, ident_set, 1)
            prologue(0)
            wait(pe, tables_in, 16 * 5)
            scores(0, 0)
            scores(0, 1)
            batch(0, True, False)
            batch(1, True, True)
            with pe.Fori(2, B - 1) as b:
                batch(b, True, True)
            batch(B - 1, False, True)
            turn_group(B - 1, G - 1)
            epilogue(B - 1)

        @block.scalar
        def _(act):
            def split_x(n):
                wait(act, xt_in, 16 * n + 16)
                wait(act, q_done, 2 * n)
                wait(act, kv_done, n)
                act.activation(xT[0][:], xT32[:], ACT.Copy).then_inc(xs_hi, 1)

            def stage_values(n):
                wait(act, kv_done, n + 1)
                wait(act, v_set, n)
                v = bank[:, F1, :].rearrange("p (t c) -> p t c", t=TT)[:, :, KW:]
                act.activation(v32[:].rearrange("p t g d -> p t (g d)"), v, ACT.Copy).then_inc(v_staged, 1)

            def set_values(n):
                wait(act, v_staged, n + 1)
                wait(act, pv_done, NP * n)
                act.activation(V[:, :, :, 0:HD], v32[:], ACT.Copy).then_inc(v_set, 1)

            def queries_turned(n, k, t):
                wait(act, q_turned, 8 * n + QI[k, t] + 1)
                wait(act, s_done, NP * n - NP + 4 * k + 4 if not (isinstance(n, int) and n == 0) else 0)
                act.activation(QT[:, 4 * k:4 * k + 4, tok(t)], bank[:, QB[k, t], :].rearrange("p (j t) -> p j t", j=4), ACT.Copy).then_inc(qt_done, 1)

            def keys_turned(n, k, t):
                wait(act, k_turned, 4 * n + 2 * k + t + 1)
                wait(act, s_done, NP * n - NP + 8 * k + 8 if not (isinstance(n, int) and n == 0) else 0)
                act.activation(KZ[0:64, 4 * k:4 * k + 4, 0, tok(t)], bank[0:64, KB[k, t], :].rearrange("p (j t) -> p j t", j=4),
                               ACT.Copy).then_inc(kz_top, 1)

            def exponentials(n, i):
                N, st = NP * n + i, i % 2
                for j in range(4):
                    h = j // 2
                    wait(act, masked, 4 * N + j + 1)
                    t = p[:, st, h, 0:2 * P] if j % 2 == 0 else p[:, st, h, 2 * P:]
                    act.activation(t, t, ACT.Exp, bias=nmax[:, st, j:j + 1], scale=-1.0).then_inc(exp_done, 1)

            def turned(n, i):
                N, st = NP * n + i, i % 2
                wait(act, p_turned, 2 * N + 1)
                wait(act, pv_done, N - 1)
                act.activation(pT[:, st, 0:4 * P], bank[:, 2 * st, :], ACT.Copy).then_inc(pT0_done, 1)

            def group(n, g):
                wait(act, pv_done, NP * n + 2 * g + 2)
                wait(act, o_turned, G * n + g)
                act.activation(ot[:], bank[:, OB, 0:S], ACT.Copy).then_inc(ot_done, 1)

            def high(dst, sem_in, value, sem_out, b, t, free):
                wait(act, sem_in, value)
                for f in free:
                    wait(act, *f)
                act.activation(dst[:, :, tok(t)], kt_view(bank[:, b, :]), ACT.Copy).then_inc(sem_out, 1)

            def x1_full(m, t):
                high(x1T32, x1_turned, 2 * m + 1 + t, x1_32, (F2, F0)[t], t, [(lr_done, m), (x1_lo, 2 * m)])

            def x1_high(m, t):
                high(x1T[0], x1_turned, 2 * m + 1 + t, x1_hi, (F2, F0)[t], t, [(z_done, 2 * m)])

            def weighted(m):
                wait(act, hw_turned, m + 1)
                wait(act, z_done, 2 * m)
                act.activation(hwT[0][:], bank[:, F0, 0:S], ACT.Copy).then_inc(hwT_hi, 1)

            def x2_high(m, t):
                high(x2T[0], x2_turned, 2 * m + 1 + t, x2_hi, (F1, F2)[t], t, [(x2T_stored, 32 * m), (w_lo, KT + 3)])

            def outputs_high(m, t):
                high(OT[0], oT_turned, 2 * m + 1 + t, oT_hi, F2, t, [(r_done, 2 * m)])

            def split_next(n):
                if not (isinstance(n, int) and n + 1 >= B):
                    split_x(n + 1)

            def split_late(i):
                dst, src = ((Wo[0][:], raw[:, :, 0:D]), (Wb[0][:], raw[:, :, 0:D]), (Lb[0][:], raw[:, 0, 0:D]))[i]
                wait(act, raw_in, 16 * i + 16)
                act.activation(dst, src, ACT.Copy).then_inc(w_hi, 1)

            def batch(b, heads, tails):
                m, n, first = b - 1, b + 1, isinstance(b, int) and b == 0
                for i in range(NP):
                    if i == 13:
                        if heads:
                            queries_turned(n, 0, 1)
                    if i % 2 == 0 and i > 0:
                        group(b, i // 2 - 1)
                    if i == 0 and not first:
                        group(m, G - 1)
                    if i == 0:
                        set_values(b)
                    if i == 0:
                        queries_turned(b, 3, 1)
                    if i == 6:
                        if first:
                            split_late(0)
                    if i == 9:
                        if first:
                            split_late(1)
                    if i == 14:
                        if heads:
                            queries_turned(n, 1, 1)
                    turned(b, i)
                    if i == 0:
                        keys_turned(b, 1, 0)
                    if i == 7:
                        if heads:
                            keys_turned(n, 0, 0)
                    if i + 1 < NP:
                        exponentials(b, i + 1)
                    elif heads:
                        exponentials(n, i + 1 - NP)
                    if i == 0:
                        if tails:
                            outputs_high(m, 0)
                    if i == 1:
                        keys_turned(b, 1, 1)
                    if i == 2:
                        if tails:
                            outputs_high(m, 1)
                    if i == 3:
                        if heads:
                            stage_values(n)
                    if i == 6:
                        if heads:
                            queries_turned(n, 0, 0)
                    if i == 7:
                        if heads:
                            queries_turned(n, 1, 0)
                    if i == 8:
                        if tails:
                            x1_full(m, 0)
                            x1_high(m, 0)
                            x1_high(m, 1)
                            x1_full(m, 1)
                    if i == 9:
                        if heads:
                            keys_turned(n, 0, 1)
                    if i == 11:
                        if heads:
                            split_next(n)
                        if tails:
                            weighted(m)
                    if i == 12:
                        if first:
                            split_late(2)
                    if i == 14:
                        if heads:
                            queries_turned(n, 2, 0)
                            queries_turned(n, 2, 1)
                    if i == 15:
                        if tails:
                            x2_high(m, 0)
                            x2_high(m, 1)
                        if heads:
                            queries_turned(n, 3, 0)

            def prologue(n):
                stage_values(n)
                queries_turned(n, 0, 0)
                keys_turned(n, 0, 0)
                queries_turned(n, 1, 0)
                keys_turned(n, 0, 1)
                split_next(n)
                queries_turned(n, 0, 1)
                queries_turned(n, 1, 1)
                queries_turned(n, 2, 0)
                queries_turned(n, 2, 1)
                queries_turned(n, 3, 0)

            def epilogue(m):
                outputs_high(m, 0)
                outputs_high(m, 1)
                x1_full(m, 0)
                x1_high(m, 0)
                x1_high(m, 1)
                x1_full(m, 1)
                weighted(m)
                x2_high(m, 0)
                x2_high(m, 1)

            split_x(0)
            for kt in range(KT):
                wait(act, qkv_in[kt], 16)
                act.activation(Wqkv[0][:, kt], raw[:, kt], ACT.Copy).then_inc(w_hi, 1)
                if kt == 0:
                    wait(act, consts_in, 16 * 3)
                    act.activation(ident_r[:], ident[:], ACT.Copy).then_inc(ident_set, 1)
            prologue(0)
            exponentials(0, 0)
            batch(0, True, False)
            batch(1, True, True)
            with act.Fori(2, B - 2) as b:
                batch(b, True, True)
            batch(B - 2, True, True)
            batch(B - 1, False, True)
            group(B - 1, G - 1)
            epilogue(B - 1)

        @block.vector
        def _(dve):
            def rotate_queries(n, t):
                wait(dve, q_done, 2 * n + 1 + t)
                wait(dve, q_lo, 2 * n + t)
                x = bank[:, (F0, F1)[t], :].rearrange("p (h d) -> p h d", h=H)
                dve.tensor_tensor(rq[:], x, cos[:, t].unsqueeze(1).to_broadcast([P, H, HD]), ALU.mult)
                dve.tensor_tensor(tq[:, :, 0:HP], x[:, :, HP:], sin[:, t, 0:HP].unsqueeze(1).to_broadcast([P, H, HP]), ALU.mult)
                dve.tensor_tensor(tq[:, :, HP:], x[:, :, 0:HP], sin[:, t, HP:].unsqueeze(1).to_broadcast([P, H, HP]), ALU.mult).then_inc(q_parts, 1)

            def rotate_keys(n):
                wait(dve, kv_done, n + 1)
                wait(dve, v_staged, n + 1)
                wait(dve, k_lo, n)
                for t in range(TT):
                    x = bank[:, F1, t * S:t * S + KW].rearrange("p (h d) -> p h d", h=G)
                    dve.tensor_tensor(rk[:, t], x, cos[:, t].unsqueeze(1).to_broadcast([P, G, HD]), ALU.mult)
                    dve.tensor_tensor(tk[:, t, :, 0:HP], x[:, :, HP:], sin[:, t, 0:HP].unsqueeze(1).to_broadcast([P, G, HP]), ALU.mult)
                    mm = dve.tensor_tensor(tk[:, t, :, HP:], x[:, :, 0:HP], sin[:, t, HP:].unsqueeze(1).to_broadcast([P, G, HP]), ALU.mult)
                mm.then_inc(k_parts, 1)

            def keys_turned(n, k, t):
                wait(dve, k_turned, 4 * n + 2 * k + t + 1)
                wait(dve, kz_top, 4 * n + 2 * k + t + 1)
                wait(dve, s_done, NP * n - NP + 8 * k + 8 if not (isinstance(n, int) and n == 0) else 0)
                dve.tensor_copy(KZ[64:128, 4 * k:4 * k + 4, 1, tok(t)], bank[64:128, KB[k, t], :].rearrange("p (j t) -> p j t", j=4))\
                    .then_inc(kz_bottom, 1)

            def mask_scores(n, i):
                N, st = NP * n + i, i % 2
                wait(dve, s_done, N + 1)
                wait(dve, gate_passed, N)
                dve.memset(gate[:, 0:1], 0.0).then_inc(gate_passed, 1)
                for j in range(4):
                    h = j // 2
                    if j % 2 == 0:
                        t, src, msk = p[:, st, h, 0:2 * P], bank[:, 2 * st, h * S:(h + 1) * S], mask[:]
                    else:
                        t, src, msk = p[:, st, h, 2 * P:], bank[:, 2 * st + 1, h * P:(h + 1) * P], mask[:, P:S]
                    dve.tensor_tensor_reduce(t, src, msk, -SCALE, BIG, ALU.add, ALU.min, nmax[:, st, j:j + 1]).then_inc(masked, 1)

            def turned(n, i):
                N, st = NP * n + i, i % 2
                wait(dve, p_turned, 2 * N + 2)
                wait(dve, pv_done, N - 1)
                dve.tensor_scalar(pT[:, st, 4 * P:6 * P], bank[:, 2 * st + 1, 0:S], 1.0, None, ALU.mult).then_inc(pT1_done, 1)

            def group(n, g):
                wait(dve, o_turned, G * n + g + 1)
                wait(dve, oT_turned, 2 * n)
                wait(dve, o_out, G * n + g)
                o = bank[:, OB, S:].rearrange("p (t j c) -> p t j c", t=TT, j=4)
                dve.reciprocal(rinv[:], o[:, :, :, HD]).then_inc(rinv_done, 1)
                wait(dve, rinv_done, G * n + g + 1)
                dve.tensor_tensor(Oat[:, :, 4 * g:4 * g + 4], o[:, :, :, 0:HD], rinv[:].unsqueeze(3).to_broadcast([P, TT, 4, HD]),
                                  ALU.mult).then_inc(o_out, 1)

            def add_attention(m, t):
                wait(dve, r_done, 2 * m + 1 + t)
                wait(dve, x_in, 16 * m + 16)
                dve.tensor_tensor(X[:, t], bank[:, (F2, F0)[t], :], X[:, t], ALU.add).then_inc(added, 1)

            def statistics(m, k, t):
                c = 4 * m + 2 * k + t
                wait(dve, added, c + 1)
                dve.bn_stats(stats[:, t], X[:, t]).then_inc(stats_done, 1)

            def variance(m, k, t):
                c = 4 * m + 2 * k + t
                wait(dve, stats_done, c + 1)
                wait(dve, variance_gate, c)
                dve.memset(gate[:, 1:2], 0.0).then_inc(variance_gate, 1)
                dve.bn_aggr(mv[:, t], stats[:, t]).then_inc(aggr_done, 1)
                wait(dve, aggr_done, c + 1)
                dve.tensor_scalar(veps[:, t:t + 1], mv[:, t, 1:2], EPS, None, ALU.add).then_inc(veps_done, 1)

            def normalise(m, k, t):
                wait(dve, rstd_done, 4 * m + 2 * k + t + 1)
                dve.tensor_scalar(X[:, t], X[:, t], mv[:, t, 0:1], rstd[:, t:t + 1], ALU.subtract, ALU.mult).then_inc(normed, 1)

            def low(dst, b, t, sem_in, sem_out, value, free=()):
                wait(dve, sem_in, value)
                for f in free:
                    wait(dve, *f)
                dve.tensor_tensor(dst[1][:, :, tok(t)], kt_view(bank[:, b, :]), dst[0][:, :, tok(t)].bitcast(F32), ALU.subtract).then_inc(sem_out, 1)

            def logits(m):
                wait(dve, lr_done, m + 1)
                wait(dve, hw_turned, m)
                lr = bank[:, F0, :].rearrange("p (t c) -> p t c", t=TT)
                dve.tensor_tensor(z[:], lr[:, :, P:P + E], b_router[:].unsqueeze(1).to_broadcast([P, TT, E]), ALU.add).then_inc(routing_steps, 1)

            def sparsemax(m):
                c = [12 * m + 1]

                def step(ins):
                    ins.then_inc(routing_steps, 1)
                    c[0] = c[0] + 1
                    wait(dve, routing_steps, c[0])

                lr = bank[:, F0, :].rearrange("p (t c) -> p t c", t=TT)
                wait(dve, routing_steps, c[0])
                wait(dve, sorting_gate, m)
                dve.memset(gate[:, 2:3], 0.0).then_inc(sorting_gate, 1)
                for t in range(TT):
                    ins = dve.max(out=c0[:, t, 4:12], in_=z[:, t])
                step(ins)
                step(dve.tensor_tensor(c1[:, :, 4:12], c0[:, :, 4:12], c0[:, :, 3:11], ALU.add))
                step(dve.tensor_tensor(c2[:, :, 4:12], c1[:, :, 4:12], c1[:, :, 2:10], ALU.add))
                step(dve.tensor_tensor(c3[:], c2[:, :, 4:12], c2[:, :, 0:8], ALU.add))
                step(dve.tensor_scalar(c3[:], c3[:], 1.0, None, ALU.subtract))
                step(dve.tensor_tensor(c3[:], c3[:], invk[:].unsqueeze(1).to_broadcast([P, TT, E]), ALU.mult))
                step(dve.tensor_reduce(tau[:], c3[:], AX.X, ALU.max))
                step(dve.tensor_tensor(z[:], z[:], tau[:].unsqueeze(2).to_broadcast([P, TT, E]), ALU.subtract))
                step(dve.tensor_scalar(z[:], z[:], 0.0, None, ALU.max))
                for t in range(TT):
                    step(dve.tensor_tensor(hw[:, t].rearrange("p (e r) -> p e r", e=E), lr[:, t, 0:P].rearrange("p (e r) -> p e r", e=E),
                                           z[:, t].unsqueeze(2).to_broadcast([P, E, R]), ALU.mult))
                assert not isinstance(m, int) or c[0] == 12 * m + 12
                dve.tensor_scalar(z[:], z[:], 0.0, None, ALU.max).then_inc(hw_done, 1)

            def add_feedforward(m, t):
                wait(dve, z_done, 2 * m + 1 + t)
                wait(dve, b_added, 2 * m + 1 + t)
                dve.tensor_tensor(X[:, t], bank[:, (F1, F2)[t], :], X[:, t], ALU.add).then_inc(added, 1)

            def outputs_low(m, t):
                low(OT, F2, t, oT_hi, oT_lo, 2 * m + 1 + t)

            def x2_low(m, t):
                low(x2T, (F1, F2)[t], t, x2_hi, x2_lo, 2 * m + 1 + t)

            def weighted_low(m):
                wait(dve, hwT_hi, m + 1)
                dve.tensor_tensor(hwT[1][:], bank[:, F0, 0:S], hwT[0][:].bitcast(F32), ALU.subtract).then_inc(hwT_lo, 1)

            def batch(b, heads, tails):
                m, n, first = b - 1, b + 1, isinstance(b, int) and b == 0
                for i in range(NP):
                    if i + 1 < NP:
                        mask_scores(b, i + 1)
                    elif heads:
                        mask_scores(n, i + 1 - NP)
                    turned(b, i)
                    if i == 8:
                        if tails:
                            normalise(m, 0, 1)
                    if i == 9:
                        if tails:
                            logits(m)
                        if heads:
                            keys_turned(n, 0, 1)
                    if i == 12:
                        if tails:
                            weighted_low(m)
                    if i == 13:
                        if tails:
                            add_feedforward(m, 1)
                    if i % 2 == 0 and i > 0:
                        group(b, i // 2 - 1)
                    if i == 0 and not first:
                        group(m, G - 1)
                    if i == 0:
                        keys_turned(b, 1, 0)
                    if i == 1:
                        if tails:
                            outputs_low(m, 0)
                        keys_turned(b, 1, 1)
                    if i == 2:
                        if tails:
                            outputs_low(m, 1)
                        if heads:
                            rotate_queries(n, 0)
                    if i == 4:
                        if heads:
                            rotate_keys(n)
                        if tails:
                            add_attention(m, 0)
                    if i == 5:
                        if tails:
                            statistics(m, 0, 0)
                            variance(m, 0, 0)
                    if i == 6:
                        if tails:
                            add_attention(m, 1)
                            statistics(m, 0, 1)
                    if i == 7:
                        if tails:
                            variance(m, 0, 1)
                            normalise(m, 0, 0)
                        if heads:
                            keys_turned(n, 0, 0)
                    if i == 8:
                        if heads:
                            rotate_queries(n, 1)
                    if i == 10:
                        if tails:
                            sparsemax(m)
                    if i == 12:
                        if tails:
                            add_feedforward(m, 0)
                            statistics(m, 1, 0)
                    if i == 13:
                        if tails:
                            variance(m, 1, 0)
                            statistics(m, 1, 1)
                    if i == 14:
                        if tails:
                            variance(m, 1, 1)
                            normalise(m, 1, 0)
                            normalise(m, 1, 1)
                    if i == 15:
                        if tails:
                            x2_low(m, 0)
                            x2_low(m, 1)

            def prologue(n):
                rotate_queries(n, 0)
                rotate_keys(n)
                stack_keys(n)
                keys_turned(n, 0, 0)
                rotate_queries(n, 1)
                stack_queries(n, 1)
                keys_turned(n, 0, 1)

            def epilogue(m):
                outputs_low(m, 0)
                outputs_low(m, 1)
                add_attention(m, 0)
                statistics(m, 0, 0)
                variance(m, 0, 0)
                add_attention(m, 1)
                statistics(m, 0, 1)
                variance(m, 0, 1)
                normalise(m, 0, 0)
                normalise(m, 0, 1)
                logits(m)
                sparsemax(m)
                weighted_low(m)
                add_feedforward(m, 0)
                statistics(m, 1, 0)
                add_feedforward(m, 1)
                variance(m, 1, 0)
                statistics(m, 1, 1)
                variance(m, 1, 1)
                normalise(m, 1, 0)
                normalise(m, 1, 1)
                x2_low(m, 0)
                x2_low(m, 1)

            for k, t in enumerate((c0, c1, c2)):
                ins = dve.memset(t[:], 0.0)
            ins = dve.memset(tau[:], 0.0)
            ins.then_inc(dve_zeroed, 1)
            wait(dve, xs_hi, 1)
            dve.tensor_tensor(xT[1][:], xT32[:], xT[0][:].bitcast(F32), ALU.subtract).then_inc(xs_lo, 1)
            for kt in range(KT):
                wait(dve, w_hi, kt + 1)
                dve.tensor_tensor(Wqkv[1][:, kt], raw[:, kt], Wqkv[0][:, kt].bitcast(F32), ALU.subtract).then_inc(w_lo, 1)
            wait(dve, dve_zeroed, 1)
            wait(dve, zeroed, 3)
            wait(dve, consts_in, 16 * 3)
            stack_queries, stack_keys = stackers(dve)
            prologue(0)
            wait(dve, tables_in, 16 * 5)
            mask_scores(0, 0)
            batch(0, True, False)
            batch(1, True, True)
            with dve.Fori(2, B - 1) as b:
                batch(b, True, True)
            batch(B - 1, False, True)
            group(B - 1, G - 1)
            epilogue(B - 1)

        @block.gpsimd
        def _(pool):
            def split_x(n):
                wait(pool, xs_hi, n + 1)
                pool.tensor_tensor(xT[1][:], xT32[:], xT[0][:].bitcast(F32), ALU.subtract).then_inc(xs_lo, 1)

            stack_queries, stack_keys = stackers(pool)

            def rescale(m, k, t):
                c = 4 * m + 2 * k + t
                wait(pool, veps_done, c + 1)
                pool.tensor_tensor(rstd[:, t:t + 1], veps[:, t:t + 1], mhalf[:], ALU.pow).then_inc(rstd_done, 1)

            def x1_low(m, t):
                wait(pool, x1_hi, 2 * m + 1 + t)
                wait(pool, x1_32, 2 * m + 1 + t)
                wait(pool, z_done, 2 * m)
                pool.tensor_tensor(x1T[1][:, :, tok(t)], x1T32[:, :, tok(t)], x1T[0][:, :, tok(t)].bitcast(F32), ALU.subtract).then_inc(x1_lo, 1)

            def add_bias(m, t):
                wait(pool, x1_turned, 2 * m + 1 + t)
                pool.tensor_tensor(X[:, t], X[:, t], b_base[:], ALU.add).then_inc(b_added, 1)

            def split_next(n):
                if not (isinstance(n, int) and n + 1 >= B):
                    split_x(n + 1)

            def split_late(i):
                dst, src, hi = ((Wo[1][:], raw[:, :, 0:D], Wo[0][:]), (Wb[1][:], raw[:, :, 0:D], Wb[0][:]),
                                (Lb[1][:], raw[:, 0, 0:D], Lb[0][:]))[i]
                wait(pool, w_hi, KT + i + 1)
                pool.tensor_tensor(dst, src, hi.bitcast(F32), ALU.subtract).then_inc(w_lo, 1)

            def batch(b, heads, tails):
                m, n, first = b - 1, b + 1, isinstance(b, int) and b == 0
                for i in range(NP):
                    if i == 0:
                        if heads:
                            stack_queries(n, 0)
                    if i == 3:
                        if heads:
                            stack_keys(n)
                    if i == 4:
                        if tails:
                            rescale(m, 0, 0)
                    if i == 5:
                        if tails:
                            rescale(m, 0, 1)
                    if i == 7:
                        if first:
                            split_late(0)
                            split_late(1)
                        if tails:
                            add_bias(m, 0)
                    if i == 8:
                        if tails:
                            x1_low(m, 0)
                            x1_low(m, 1)
                    if i == 10:
                        if tails:
                            add_bias(m, 1)
                    if i == 11:
                        if heads:
                            stack_queries(n, 1)
                        if first:
                            split_late(2)
                    if i == 12:
                        if heads:
                            split_next(n)
                    if i == 14:
                        if tails:
                            rescale(m, 1, 0)
                    if i == 15:
                        if tails:
                            rescale(m, 1, 1)

            def prologue(n):
                stack_queries(n, 0)
                split_next(n)

            def epilogue(m):
                rescale(m, 0, 0)
                rescale(m, 0, 1)
                add_bias(m, 0)
                x1_low(m, 0)
                x1_low(m, 1)
                add_bias(m, 1)
                rescale(m, 1, 0)
                rescale(m, 1, 1)

            pool.memset(KZ[:].bitcast(F32), 0.0).then_inc(zeroed, 1)
            pool.memset(V[:], 0.0).then_inc(zeroed, 1)
            pool.memset(mhalf[:], -0.5).then_inc(zeroed, 1)
            wait(pool, zeroed, 3)
            pool.memset(V[:, :, :, HD:HD + 1], 1.0).then_inc(zeroed, 1)
            wait(pool, zeroed, 4)
            prologue(0)
            wait(pool, tables_in, 16 * 5)
            batch(0, True, False)
            batch(1, True, True)
            with pool.Fori(2, B - 2) as b:
                batch(b, True, True)
            batch(B - 2, True, True)
            batch(B - 1, False, True)
            epilogue(B - 1)


def attention1(nc, x2, x2T_hi, x2T_lo, w_attn, w_ffn, b2_row, cos, sin, mask, ident, stage, early, rows_t, raw1, b2, Y, x2T_stored):
    G, HG, HD = 8, 4, 128
    STEPS = G * B
    SCALE = float(np.float32(1.0 / np.sqrt(HD)))
    KV, QO = 2 * KT * HD, KT * HG * HD
    with ExitStack() as ctx:
        def sb(name, shape, dt=F32):
            return ctx.enter_context(nc.sbuf_tensor("a1_" + name, shape, dt))

        def sem(name):
            return ctx.enter_context(nc.semaphore("a1_" + name))

        def pair(name, shape):
            return sb(name + "_hi", shape, F32R), sb(name + "_lo", shape, F32R)

        raw = stage[:].bitcast(F32)
        XT = pair("XT", [P, B - 1, KT, S])
        Wk, Wv = pair("Wk", [P, KT, HD]), pair("Wv", [P, KT, HD])
        Wq, Wo = pair("Wq", [P, KT, HG * HD]), pair("Wo", [P, HG, D])
        q32, q, tmp = rows_t[:, 0:HG * S].rearrange("p (h t) -> p h t", h=HG), pair("q", [P, HG, S]), sb("tmp", [P, HG + 1, S])
        k32, k = sb("k32", [P, S]), pair("k", [P, S])
        vT, V = sb("vT", [P, S]), pair("V", [P, TT, HD])
        p = rows_t[:, HG * S:HG * S + 3 * HG * P].rearrange("p (h t) -> p h t", h=HG)
        pT = pair("pT", [P, 3 * HG * P])
        o = pair("o", [P, HG, S])
        stats, mv = sb("stats", [P, TT, 6]), sb("mv", [P, TT, 2])
        veps, rstd, mhalf, gates = sb("veps", [P, TT]), sb("rstd", [P, TT]), sb("mhalf", [P, TT]), sb("gates", [P, 2])
        nmax, rsum, rinv = sb("nmax", [P, 2 * HG]), sb("rsum", [P, 2 * HG]), sb("rinv", [P, 2 * HG])
        bank = ctx.enter_context(nc.psum_tensor("a1_bank", [P, 8, D], F32))
        Q0, KVB, S0, SQ0, Y0 = 0, 2, 3, 5, 6

        ffn_in, xt_in = sem("ffn_in"), [sem(f"xt_in{i}") for i in range(4)]
        y_in, raw_in = sem("y_in"), sem("raw_in")
        w_hi, wkv_lo, wq0_lo, wq1_lo, wo_lo = sem("w_hi"), sem("wkv_lo"), sem("wq0_lo"), sem("wq1_lo"), sem("wo_lo")
        kv_done, q_done, v_turned = sem("kv_done"), sem("q_done"), sem("v_turned")
        s_done, p_turned, o_done, y_done = sem("s_done"), sem("p_turned"), sem("o_done"), sem("y_done")
        vT_copied, v_hi, k_hi, q_hi = sem("vT_copied"), sem("v_hi"), sem("k_hi"), sem("q_hi")
        exp_done, pT_hi, o_hi = sem("exp_done"), sem("pT_hi"), sem("o_hi")
        v_lo, masked, rinv_done, p_ready = sem("v_lo"), sem("masked"), sem("rinv_done"), sem("p_ready")
        k_parts, q_parts, pT_lo, o_lo, y_added = sem("k_parts"), sem("q_parts"), sem("pT_lo"), sem("o_lo"), sem("y_added")
        stats_done, aggr_done, veps_done, rstd_done, normed, mhalf_set = (
            sem("stats_done"), sem("aggr_done"), sem("veps_done"), sem("rstd_done"), sem("normed"), sem("mhalf_set"))
        k_rot, q_rot, k_lo, q_lo = sem("k_rot"), sem("q_rot"), sem("k_lo"), sem("q_lo")

        block = ctx.enter_context(nc.Block())
        wa = w_attn

        kv_parts = ((Wk, slice(0, KT), 0, KV // 2), (Wv, slice(0, KT), KV // 2, KV))
        q_parts_of = ((Wq, slice(0, KT // 2), KV, KV + QO // 2), (Wq, slice(KT // 2, KT), KV + QO // 2, KV + QO))
        o_part = (Wo, slice(0, HG), 0, QO)

        def flat(half, part):
            w, kts = part[0], part[1]
            return w[half][:, kts].rearrange("p a b -> p (a b)")

        def staged(part, g):
            if part in q_parts_of and isinstance(g, int) and g == 0:
                return rows_t[:, part[2] - KV:part[3] - KV]
            return raw[:, part[2]:part[3]]

        def low_half(eng, part, g):
            return eng.tensor_tensor(flat(1, part), staged(part, g), flat(0, part).bitcast(F32), ALU.subtract)

        def rotate_queries(eng, n, i):
            hs = slice(2 * i, 2 * i + 2)
            eng.wait_ge(q_parts, 2 * n + 1 + i)
            eng.tensor_tensor(q32[:, hs, :], q32[:, hs, :], tmp[:, hs, :], ALU.add).then_inc(q_rot, 1)
            eng.wait_ge(q_hi, 2 * n + 1 + i)
            eng.tensor_tensor(q[1][:, hs, :], q32[:, hs, :], q[0][:, hs, :].bitcast(F32), ALU.subtract).then_inc(q_lo, 1)

        @block.sync
        def _(sp):
            sp.wait_ge(x2T_stored, 32 * B)
            for b in range(1, B):
                for half, src in zip(XT, (x2T_hi, x2T_lo)):
                    sp.dma_start(half[:, b - 1].bitcast(F32), src[:, b]).then_inc(xt_in[min(b, 3)], 16)
                if b == 1:
                    sp.wait_ge(wkv_lo, 1)
                    sp.dma_start(raw[:, 0:QO], wa[:, 0, KV + QO:]).then_inc(raw_in, 16)
                if b == 2:
                    sp.dma_start(Y[:], x2).then_inc(y_in, 16)
            sp.dma_start(raw1[:], w_ffn[:, 0, 0:raw1.shape[1]]).then_inc(ffn_in, 16)
            sp.dma_start(b2[:], b2_row.partition_broadcast(P)).then_inc(ffn_in, 16)
            with sp.Fori(1, G) as g:
                sp.wait_ge(wo_lo, g)
                sp.dma_start(raw, wa[:, g, 0:KV + QO]).then_inc(raw_in, 16)
                sp.wait_ge(wkv_lo, g + 1)
                sp.wait_ge(wq0_lo, g + 1)
                sp.wait_ge(wq1_lo, g + 1)
                sp.dma_start(raw[:, 0:QO], wa[:, g, KV + QO:]).then_inc(raw_in, 16)
            sp.wait_ge(ffn_in, 32)

        @block.tensor
        def _(pe):
            def project(n, b, g):
                pe.wait_ge(wkv_lo, g + 1)

                def xT(kt):
                    if isinstance(b, int) and b == 0:
                        return early[:, 0, kt], early[:, 1, kt]
                    return halves(XT, slice(None), b - 1, kt)

                if not isinstance(n, int) or n >= 1:
                    pe.wait_ge(v_lo, n)
                for i, w in enumerate((Wk, Wv)):
                    for kt in range(KT):
                        mm = product(pe, bank[:, KVB, i * S:(i + 1) * S], halves(w, slice(None), kt), xT(kt),
                                     kt == 0, kt == KT - 1)
                mm.then_inc(kv_done, 1)
                pe.wait_ge(wq0_lo, g + 1)
                pe.wait_ge(wq1_lo, g + 1)
                for h in range(HG):
                    if h % 2 == 0 and (not isinstance(n, int) or n >= 2):
                        pe.wait_ge(o_lo, 2 * n - 3 + h // 2)
                    for kt in range(KT):
                        mm = product(pe, bank[:, Q0 + h // 2, h % 2 * S:(h % 2 + 1) * S],
                                     halves(Wq, slice(None), kt, slice(h * HD, (h + 1) * HD)), xT(kt),
                                     kt == 0, kt == KT - 1)
                    if h % 2:
                        mm.then_inc(q_done, 1)

            def scores(m):
                pe.wait_ge(k_parts, m + 1)
                pe.wait_ge(vT_copied, m + 1)
                for tt in range(TT):
                    mm = pe.transpose(bank[:, KVB, tt * P:(tt + 1) * P], vT[:, tt * P:(tt + 1) * P], ident[:])
                mm.then_inc(v_turned, 1)
                pe.wait_ge(k_lo, m + 1)
                pe.wait_ge(q_lo, 2 * m + 2)
                first = isinstance(m, int) and m == 0
                if not first:
                    pe.wait_ge(pT_lo, 3 * m)
                for h in range(HG):
                    mm = pe.matmul(bank[:, SQ0, h * P:(h + 1) * P], q32[:, h, 0:P], k32[:, 0:P], start=True, stop=True)
                mm.then_inc(s_done, 1)
                for h in range(HG):
                    mm = product(pe, bank[:, S0 + h // 2, h % 2 * S:(h % 2 + 1) * S],
                                 halves(q, slice(None), h, slice(P, S)), halves(k, slice(None)))
                    if h % 2:
                        mm.then_inc(s_done, 1)

            def turn(m):
                pe.wait_ge(p_ready, 8 * m + 8)
                for h in range(HG):
                    dst = bank[:, S0 + h // 2, h % 2 * S:(h % 2 + 1) * S]
                    pe.transpose(dst[:, 0:P], p[:, h, 2 * P:3 * P], ident[:])
                    mm = pe.transpose(dst[:, P:S], p[:, h, 0:P], ident[:])
                    if h % 2:
                        mm.then_inc(p_turned, 1)
                for h in range(HG):
                    mm = pe.transpose(bank[:, SQ0, h * P:(h + 1) * P], p[:, h, P:2 * P], ident[:])
                mm.then_inc(p_turned, 1)

            def rows(m, g):
                pe.wait_ge(wo_lo, g + 1)
                for tt in range(TT):
                    if not (isinstance(m, int) and m == 0):
                        pe.wait_ge(y_added, 2 * m - 1 + tt)
                    for h in range(HG):
                        if tt == 0 and h % 2 == 0:
                            pe.wait_ge(o_lo, 2 * m + 1 + h // 2)
                        mm = product(pe, bank[:, Y0 + tt, :], halves(o, slice(None), h, slice(tt * P, (tt + 1) * P)),
                                     halves(Wo, slice(None), h), h == 0, h == HG - 1)
                    mm.then_inc(y_done, 1)

            def values(m, last=False):
                pe.wait_ge(v_lo, m + 1)
                for i in range(2):
                    pe.wait_ge(pT_lo, 3 * m + 1 + i)
                    if not last:
                        pe.wait_ge(q_parts, 2 * m + 3 + i)
                    product(pe, bank[:, Q0 + i, :], halves(V, slice(None), 0), halves(pT, slice(None), slice(i * 512, i * 512 + 512)),
                            True, False)
                pe.wait_ge(pT_lo, 3 * m + 3)
                for i in range(2):
                    out = bank[:, Q0 + i, :].rearrange("p (h s) -> p h s", h=2)[:, :, P:S]
                    x = halves(pT, slice(None), slice(1024 + i * 256, 1024 + i * 256 + 256))
                    x = tuple(a.rearrange("p (h s) -> p h s", h=2) for a in x)
                    mm = product(pe, out, halves(V, slice(None), 1), x, False, True)
                    mm.then_inc(o_done, 1)

            def step(n, b, g, g_rows):
                scores(n - 1)
                project(n, b, g)
                turn(n - 1)
                if not isinstance(n, int) or n >= 2:
                    rows(n - 2, g_rows)
                values(n - 1)

            project(0, 0, 0)
            pe.wait_ge(xt_in[1], 32)
            step(1, 1, 0, 0)
            pe.wait_ge(xt_in[2], 32)
            step(2, 2, 0, 0)
            pe.wait_ge(xt_in[3], 32 * (B - 3))
            with pe.Fori(3, B) as b:
                step(b, b, 0, 0)
            with pe.Fori(1, G) as g:
                step(g * B, 0, g, g - 1)
                step(g * B + 1, 1, g, g - 1)
                with pe.Fori(2, B) as b:
                    step(g * B + b, b, g, g)
            scores(STEPS - 1)
            rows(STEPS - 2, G - 1)
            turn(STEPS - 1)
            values(STEPS - 1, last=True)
            rows(STEPS - 1, G - 1)

        @block.scalar
        def _(act):
            def high_half(part, g):
                return act.activation(flat(0, part), staged(part, g), ACT.Copy)

            def split_qkv(g, first=False):
                if not first:
                    act.wait_ge(kv_done, B * g)
                    act.wait_ge(raw_in, 32 * g)
                for part in kv_parts:
                    ins = high_half(part, g)
                ins.then_inc(w_hi, 1)
                if not first:
                    act.wait_ge(q_done, 2 * B * g)
                for part in q_parts_of:
                    high_half(part, g).then_inc(w_hi, 1)

            def split_wo(g, first=False):
                act.wait_ge(raw_in, 32 * g + 16)
                if not first:
                    act.wait_ge(y_done, 2 * B * g)
                high_half(o_part, g).then_inc(w_hi, 1)

            def outputs(m):
                for i in range(2):
                    act.wait_ge(o_done, 2 * m + 1 + i)
                    if i == 0 and not (isinstance(m, int) and m == 0):
                        act.wait_ge(y_done, 2 * m)
                    act.activation(o[0][:, 2 * i:2 * i + 2, :], bank[:, Q0 + i, :].rearrange("p (h s) -> p h s", h=2),
                                   ACT.Copy).then_inc(o_hi, 1)

            def softmax(m):
                act.wait_ge(v_turned, m + 1)
                if not (isinstance(m, int) and m == 0):
                    act.wait_ge(o_done, 2 * m)
                act.activation(V[0][:], bank[:, KVB, 0:S].rearrange("p (t d) -> p t d", t=TT), ACT.Copy).then_inc(v_hi, 1)
                for j in range(2 * HG):
                    act.wait_ge(masked, 8 * m + j + 1)
                    h = j % HG
                    t = p[:, h, 2 * P:3 * P] if j < HG else p[:, h, 0:2 * P]
                    act.activation(t, t, ACT.Exp, bias=nmax[:, j:j + 1], scale=-1.0,
                                   accum_out=rsum[:, j:j + 1]).then_inc(exp_done, 1)

            def projected(n):
                act.wait_ge(kv_done, n + 1)
                act.activation(vT[:], bank[:, KVB, S:2 * S], ACT.Copy).then_inc(vT_copied, 1)

            def keys(n):
                act.wait_ge(k_rot, n + 1)
                act.activation(k[0][:], k32[:], ACT.Copy).then_inc(k_hi, 1)

            def queries(n, i):
                act.wait_ge(q_rot, 2 * n + 1 + i)
                act.activation(q[0][:, 2 * i:2 * i + 2, :], q32[:, 2 * i:2 * i + 2, :], ACT.Copy).then_inc(q_hi, 1)

            def turned(m):
                for i in range(3):
                    act.wait_ge(p_turned, 3 * m + 1 + i)
                    if i == 0 and not (isinstance(m, int) and m == 0):
                        act.wait_ge(o_done, 2 * m)
                    act.activation(pT[0][:, i * D:(i + 1) * D], bank[:, S0 + i, :], ACT.Copy).then_inc(pT_hi, 1)

            def step(n):
                if not isinstance(n, int) or n >= 2:
                    outputs(n - 2)
                softmax(n - 1)
                projected(n)
                keys(n)
                if isinstance(n, int) and n == 1:
                    turned(n - 1)
                    queries(n, 0)
                else:
                    queries(n, 0)
                    turned(n - 1)
                queries(n, 1)

            split_qkv(0, first=True)
            projected(0), keys(0), queries(0, 0), queries(0, 1)
            step(1)
            split_wo(0, first=True)
            step(2)
            with act.Fori(3, B) as b:
                step(b)
            with act.Fori(1, G) as g:
                split_qkv(g)
                step(g * B)
                step(g * B + 1)
                split_wo(g)
                with act.Fori(2, B) as b:
                    step(g * B + b)
            outputs(STEPS - 2)
            softmax(STEPS - 1)
            turned(STEPS - 1)
            outputs(STEPS - 1)

        @block.vector
        def _(dve):
            def split_wq(g):
                dve.wait_ge(w_hi, 4 * g + 2)
                low_half(dve, q_parts_of[0], g).then_inc(wq0_lo, 1)

            def outputs(m, i):
                dve.wait_ge(o_hi, 2 * m + 1 + i)
                dst = o[1][:, 2 * i:2 * i + 2, :]
                dve.tensor_tensor(dst, bank[:, Q0 + i, :].rearrange("p (h s) -> p h s", h=2),
                                  o[0][:, 2 * i:2 * i + 2, :].bitcast(F32), ALU.subtract).then_inc(o_lo, 1)

            def scored(m, outputs_of=None):
                if outputs_of is not None:
                    outputs(outputs_of, 0)
                if not (isinstance(m, int) and m == 0):
                    dve.wait_ge(p_turned, 3 * m)
                dve.wait_ge(s_done, 3 * m + 1)
                dve.wait_ge(v_hi, m + 1)
                dve.tensor_tensor(V[1][:], bank[:, KVB, 0:S].rearrange("p (t d) -> p t d", t=TT),
                                  V[0][:].bitcast(F32), ALU.subtract).then_inc(v_lo, 1)
                for j in range(2 * HG):
                    h = j % HG
                    if j == HG:
                        dve.wait_ge(s_done, 3 * m + 3)
                        if outputs_of is not None:
                            outputs(outputs_of, 1)
                    if j < HG:
                        t, src, msk = p[:, h, 2 * P:3 * P], bank[:, SQ0, h * P:(h + 1) * P], mask[:, P:S]
                    else:
                        t, src, msk = p[:, h, 0:2 * P], bank[:, S0 + h // 2, h % 2 * S:(h % 2 + 1) * S], mask[:]
                    dve.tensor_tensor_reduce(t, src, msk, -SCALE, BIG, ALU.add, ALU.min,
                                             nmax[:, j:j + 1]).then_inc(masked, 1)

            def normalised(m):
                for half in range(2):
                    c = slice(half * HG, half * HG + HG)
                    dve.wait_ge(exp_done, 8 * m + 4 * half + 4)
                    dve.reciprocal(rinv[:, c], rsum[:, c]).then_inc(rinv_done, 1)
                    dve.wait_ge(rinv_done, 2 * m + half + 1)
                    for h in range(HG):
                        t = p[:, h, 0:2 * P] if half else p[:, h, 2 * P:3 * P]
                        dve.tensor_scalar(t, t, rinv[:, half * HG + h:half * HG + h + 1], None, ALU.mult).then_inc(p_ready, 1)

            def rotate(out, tmp_t, src, heads):
                c = cos[:].unsqueeze(1).to_broadcast([P, heads, S])
                s_lo = sin[0:64].unsqueeze(1).to_broadcast([64, heads, S])
                s_hi = sin[64:128].unsqueeze(1).to_broadcast([64, heads, S])
                dve.tensor_tensor(out, src, c, ALU.mult)
                dve.tensor_tensor(tmp_t[0:64], src[64:128], s_lo, ALU.mult)
                return dve.tensor_tensor(tmp_t[64:128], src[0:64], s_hi, ALU.mult)

            def keys(n):
                dve.wait_ge(vT_copied, n + 1)
                if not isinstance(n, int) or n >= 1:
                    dve.wait_ge(s_done, 3 * n)
                    dve.wait_ge(k_lo, n)
                rotate(k32[:].unsqueeze(1), tmp[:, HG:HG + 1, :], bank[:, KVB, 0:S].unsqueeze(1), 1).then_inc(k_parts, 1)

            def queries(n, i):
                dve.wait_ge(q_done, 2 * n + 1 + i)
                if not isinstance(n, int) or n >= 1:
                    dve.wait_ge(q_lo, 2 * n)
                hs = slice(2 * i, 2 * i + 2)
                rotate(q32[:, hs, :], tmp[:, hs, :], bank[:, Q0 + i, :].rearrange("p (h s) -> p h s", h=2), 2)\
                    .then_inc(q_parts, 1)

            def turned(m):
                for i in range(3):
                    dve.wait_ge(pT_hi, 3 * m + 1 + i)
                    c = slice(i * D, (i + 1) * D)
                    dve.tensor_tensor(pT[1][:, c], bank[:, S0 + i, :], pT[0][:, c].bitcast(F32), ALU.subtract).then_inc(pT_lo, 1)

            def accumulate(m, b):
                for tt in range(TT):
                    dve.wait_ge(y_done, 2 * m + 1 + tt)
                    y = Y[:, TT * b + tt, :]
                    dve.tensor_tensor(y, bank[:, Y0 + tt, :], y, ALU.add).then_inc(y_added, 1)

            def gate(scratch):
                dve.memset(scratch, 0.0)

            def statistics(b):
                dve.wait_ge(y_added, 2 * ((G - 1) * B + b) + 2)
                gate(gates[:, 0:1])
                for tt in range(TT):
                    dve.bn_stats(stats[:, tt, :], Y[:, TT * b + tt, :]).then_inc(stats_done, 1)
                dve.wait_ge(stats_done, TT * b + TT)
                gate(gates[:, 1:2])
                for tt in range(TT):
                    dve.bn_aggr(mv[:, tt, :], stats[:, tt, :]).then_inc(aggr_done, 1)
                dve.wait_ge(aggr_done, TT * b + TT)
                dve.tensor_scalar(veps[:], mv[:, :, 1], EPS, None, ALU.add).then_inc(veps_done, 1)

            def normalise(b):
                dve.wait_ge(rstd_done, b + 1)
                for tt in range(TT):
                    y = Y[:, TT * b + tt, :]
                    dve.tensor_scalar(y, y, mv[:, tt, 0:1], rstd[:, tt:tt + 1], ALU.subtract, ALU.mult).then_inc(normed, 1)

            def step(n, b_rows, split=None, complete=None):
                scored(n - 1, None if isinstance(n, int) and n < 2 else n - 2)
                keys(n)
                normalised(n - 1)
                queries(n, 0)
                queries(n, 1)
                if complete is not None:
                    statistics(complete)
                turned(n - 1)
                if not isinstance(n, int) or n >= 2:
                    accumulate(n - 2, b_rows)
                if split is not None:
                    split_wq(split)

            dve.wait_ge(w_hi, 1)
            for part in kv_parts:
                ins = low_half(dve, part, 0)
            ins.then_inc(wkv_lo, 1)
            split_wq(0)
            keys(0), queries(0, 0), queries(0, 1)
            dve.wait_ge(q_lo, 1)
            rotate_queries(dve, 0, 1)
            step(1, None)
            dve.wait_ge(y_in, 16)
            with dve.Fori(2, B - 1) as b:
                step(b, b - 2)
            step(B - 1, B - 3, split=1)
            with dve.Fori(1, G - 1) as g:
                step(g * B, B - 2)
                step(g * B + 1, B - 1)
                with dve.Fori(2, B - 1) as b:
                    step(g * B + b, b - 2)
                step(g * B + B - 1, B - 3, split=g + 1)
            step((G - 1) * B, B - 2)
            step((G - 1) * B + 1, B - 1)
            step((G - 1) * B + 2, 0)
            with dve.Fori(3, B) as b:
                step((G - 1) * B + b, b - 2, complete=b - 3)
                normalise(b - 3)
            scored(STEPS - 1, STEPS - 2)
            normalised(STEPS - 1)
            turned(STEPS - 1)
            accumulate(STEPS - 2, B - 2)
            outputs(STEPS - 1, 0)
            outputs(STEPS - 1, 1)
            statistics(B - 3)
            normalise(B - 3)
            accumulate(STEPS - 1, B - 1)

        @block.gpsimd
        def _(pool):
            def step(n):
                pool.wait_ge(k_parts, n + 1)
                pool.tensor_tensor(k32[:], k32[:], tmp[:, HG, :], ALU.add).then_inc(k_rot, 1)
                pool.wait_ge(k_hi, n + 1)
                pool.tensor_tensor(k[1][:], k32[:], k[0][:].bitcast(F32), ALU.subtract).then_inc(k_lo, 1)
                for i in range(1 if isinstance(n, int) and n == 0 else 2):
                    rotate_queries(pool, n, i)

            def split_qkv(g):
                if not isinstance(g, int) or g > 0:
                    pool.wait_ge(w_hi, 4 * g + 1)
                    for part in kv_parts:
                        ins = low_half(pool, part, g)
                    ins.then_inc(wkv_lo, 1)
                pool.wait_ge(w_hi, 4 * g + 3)
                low_half(pool, q_parts_of[1], g).then_inc(wq1_lo, 1)

            def split_wo(g):
                pool.wait_ge(w_hi, 4 * g + 4)
                low_half(pool, o_part, g).then_inc(wo_lo, 1)

            def group(g):
                split_qkv(g)
                step(g * B)
                step(g * B + 1)
                split_wo(g)
                with pool.Fori(2, B) as b:
                    step(g * B + b)

            def rescale(b):
                pool.wait_ge(veps_done, b + 1)
                pool.tensor_tensor(rstd[:], veps[:], mhalf[:], ALU.pow).then_inc(rstd_done, 1)

            pool.memset(mhalf[:], -0.5).then_inc(mhalf_set, 1)
            group(0)
            with pool.Fori(1, G - 1) as g:
                group(g)
            split_qkv(G - 1)
            step((G - 1) * B)
            step((G - 1) * B + 1)
            split_wo(G - 1)
            step((G - 1) * B + 2)
            pool.wait_ge(mhalf_set, 1)
            with pool.Fori(3, B) as b:
                step((G - 1) * B + b)
                rescale(b - 3)
            rescale(B - 3)


def ffn1(nc, w_ffn, ident, raw1, b2, out, Y):
    G, FT, C = 8, 2, 4
    CT = NT // C
    CB = B // C
    STEPS = G * C
    W1N, W2N = KT * FT * P, FT * D
    with ExitStack() as ctx:
        def sb(name, shape, dt=F32):
            return ctx.enter_context(nc.sbuf_tensor("f1_" + name, shape, dt))

        def sem(name):
            return ctx.enter_context(nc.semaphore("f1_" + name))

        def pair(name, shape):
            return sb(name + "_hi", shape, F32R), sb(name + "_lo", shape, F32R)

        XT, raw2 = pair("XT", [P, B, KT, S]), sb("raw2", [P, W2N])
        W1, W2, b1 = pair("W1", [P, KT, FT * P]), pair("W2", [P, FT, D]), sb("b1", [P, FT])
        h32, hs = sb("h32", [P, FT, D]), (pair("h0", [P, FT, D]), pair("h1", [P, FT, D]))
        stats, mv, mhalf = sb("stats", [P, CT, 6]), sb("mv", [P, CT, 2]), sb("mhalf", [P, CT])
        veps, rstd = sb("veps", [P, CT]), sb("rstd", [P, CT])
        nmean, shift = sb("nmean", [P, CT]), sb("shift", [P, CT])
        mv3, veps3, rstd3 = sb("mv3", [P, CT, 2]), sb("veps3", [P, CT]), sb("rstd3", [P, CT])
        bank = ctx.enter_context(nc.psum_tensor("f1_bank", [P, 8, D], F32))
        H0, Y0, X0 = 0, 2, 6

        raw1_in, raw2_in = sem("raw1_in"), sem("raw2_in")
        mhalf_set, b1_set, w1_hi, w1_lo, w2_hi, w2_lo = sem("mhalf_set"), sem("b1_set"), sem("w1_hi"), sem("w1_lo"), sem("w2_hi"), sem("w2_lo")
        stats_done, aggr_done, veps_done, rstd_done, normed = (
            sem("stats_done"), sem("aggr_done"), sem("veps_done"), sem("rstd_done"), sem("normed"))
        mean_negated, shift_set, act_normed = sem("mean_negated"), sem("shift_set"), sem("act_normed")
        x_turned, x_hi, x_lo, b2_added = sem("x_turned"), sem("x_hi"), sem("x_lo"), sem("b2_added")
        h_done, gelu_done, h_hi, h_lo = sem("h_done"), sem("gelu_done"), sem("h_hi"), sem("h_lo")
        y_done, y_added, stored = sem("y_done"), sem("y_added"), sem("stored")

        def x_bank(i):
            return Y0 + i % CT if i < 2 * CT and i % CT >= 2 else X0 + i % 2

        def tiles(c, half=None):
            return range(CT * c, CT * c + CT) if half is None else range(CT * c + 2 * half, CT * c + 2 * half + 2)

        block = ctx.enter_context(nc.Block())

        @block.sync
        def _(sp):
            sp.dma_start(raw2[:], w_ffn[:, 0, W1N + FT:]).then_inc(raw2_in, 16)
            with sp.Fori(1, G) as g:
                sp.wait_ge(w1_lo, g)
                sp.wait_ge(b1_set, g)
                sp.dma_start(raw1[:], w_ffn[:, g, 0:W1N + FT]).then_inc(raw1_in, 16)
                sp.wait_ge(w2_lo, g)
                sp.dma_start(raw2[:], w_ffn[:, g, W1N + FT:]).then_inc(raw2_in, 16)
            for i in range(NT):
                c = i // CT
                if c == C - 2:
                    sp.wait_ge(act_normed, i % CT + 1)
                else:
                    sp.wait_ge(normed, CT + i + 1 if c < C - 2 else i + 1)
                sp.dma_start(out[:, i, :], Y[:, i, :]).then_inc(stored, 16)
            sp.wait_ge(stored, 16 * NT)

        @block.tensor
        def _(pe):
            chunks = tuple(t[:].rearrange("p (c b) k t -> p c b k t", b=CB) for t in XT)

            def turn(c, half=None):
                for i in tiles(c, half):
                    if c == C - 1:
                        pe.wait_ge(normed, i - CT * c + 1)
                    if c >= 2:
                        pe.wait_ge(x_lo, i - 1)
                    for kt in range(KT):
                        mm = pe.transpose(bank[:, x_bank(i), kt * P:(kt + 1) * P], Y[:, i, kt * P:(kt + 1) * P], ident[:])
                    mm.then_inc(x_turned, 1)

            def hidden(s, c, g, turns=False):
                pe.wait_ge(w1_lo, g + 1)
                for f in range(FT):
                    if not isinstance(s, int) or s >= 1:
                        pe.wait_ge(gelu_done, FT * s - 1 + f)
                    for kt in range(KT):
                        mm = product(pe, bank[:, H0 + f, :].rearrange("p (b t) -> p b t", b=CB),
                                     halves(W1, slice(None), kt, slice(f * P, (f + 1) * P)),
                                     halves(chunks, slice(None), c, slice(None), kt), kt == 0, kt == KT - 1)
                    mm.then_inc(h_done, 1)
                    if turns and c == 0 and f == 0:
                        turn(1)
                    elif turns and c:
                        turn(c + 1, f)

            def rows(s, c, g):
                h = hs[c % 2]
                pe.wait_ge(w2_lo, g + 1)
                pe.wait_ge(h_lo, FT * s + FT)
                for t in range(CT):
                    if not isinstance(s, int) or s >= 1:
                        pe.wait_ge(y_added, CT * s - 3 + t)
                    for f in range(FT):
                        mm = product(pe, bank[:, Y0 + t, :], halves(h, slice(None), f, slice(t * P, (t + 1) * P)),
                                     halves(W2, slice(None), f), f == 0, f == FT - 1)
                    mm.then_inc(y_done, 1)

            turn(0)
            for c in range(C):
                pe.wait_ge(x_lo, CT * (c + 1))
                hidden(c, c, 0, turns=c + 1 < C)
                if c:
                    rows(c - 1, c - 1, 0)
            with pe.Fori(1, G) as g:
                for c in range(C):
                    hidden(g * C + c, c, g)
                    rows(g * C + c - 1, (c - 1) % C, g if c else g - 1)
            rows(STEPS - 1, C - 1, G - 1)

        @block.scalar
        def _(act):
            def split_w1(g):
                if not (isinstance(g, int) and g == 0):
                    act.wait_ge(raw1_in, 16 * g)
                    act.wait_ge(h_done, FT * C * g)
                act.activation(W1[0][:].rearrange("p a b -> p (a b)"), raw1[:, 0:W1N], ACT.Copy).then_inc(w1_hi, 1)

            def load_b1(g):
                act.activation(b1[:], raw1[:, W1N:W1N + FT], ACT.Copy).then_inc(b1_set, 1)

            def split_w2(g):
                act.wait_ge(raw2_in, 16 * g + 16)
                if not (isinstance(g, int) and g == 0):
                    act.wait_ge(y_done, CT * C * g)
                act.activation(W2[0][:].rearrange("p a b -> p (a b)"), raw2[:], ACT.Copy).then_inc(w2_hi, 1)

            def turned(c, half=None):
                for i in tiles(c, half):
                    act.wait_ge(x_turned, i + 1)
                    act.activation(XT[0][:, i // TT, :, i % TT * P:(i % TT + 1) * P],
                                   bank[:, x_bank(i), :].rearrange("p (k t) -> p k t", k=KT), ACT.Copy).then_inc(x_hi, 1)

            def activate(s, g, turns=False):
                for f in range(FT):
                    act.wait_ge(h_done, FT * s + f + 1)
                    act.wait_ge(b1_set, g + 1)
                    if f == 0 and not (isinstance(s, int) and s == 0):
                        act.wait_ge(h_lo, FT * s)
                    act.activation(h32[:, f, :], bank[:, H0 + f, :], ACT.Gelu_apprx_tanh, bias=b1[:, f:f + 1]).then_inc(gelu_done, 1)
                    if turns and s == 0 and f == 0:
                        turned(1)
                    elif turns and s:
                        turned(s + 1, f)

            def hidden(s, c):
                h = hs[c % 2]
                act.wait_ge(gelu_done, FT * s + FT)
                if not isinstance(s, int) or s >= 2:
                    act.wait_ge(y_done, CT * (s - 1))
                for f in range(FT):
                    act.activation(h[0][:, f, :], h32[:, f, :], ACT.Copy).then_inc(h_hi, 1)

            def group(g, more):
                for c in range(C):
                    if c == C - 1 and more:
                        split_w1(g + 1)
                    activate(g * C + c, g, turns=isinstance(g, int) and g == 0 and c + 1 < C)
                    hidden(g * C + c, c)
                    if c == 0 and not (isinstance(g, int) and g == 0):
                        split_w2(g)
                if more:
                    load_b1(g + 1)

            split_w1(0)
            turned(0)
            load_b1(0)
            split_w2(0)
            group(0, True)
            with act.Fori(1, G - 1) as g:
                group(g, True)
            group(G - 1, False)
            act.wait_ge(shift_set, 1)
            for j in range(CT):
                y = Y[:, CT * (C - 2) + j, :]
                act.activation(y, y, ACT.Identity, bias=shift[:, j:j + 1], scale=rstd[:, j:j + 1]).then_inc(act_normed, 1)

        @block.vector
        def _(dve):
            def normalise_last():
                for pr in range(CT // 2):
                    two = (2 * pr, 2 * pr + 1)
                    for j in two:
                        dve.wait_ge(y_done, CT * STEPS - CT + j + 1)
                        y = Y[:, NT - CT + j, :]
                        dve.tensor_tensor(y, bank[:, Y0 + j, :], y, ALU.add).then_inc(y_added, 1)
                    for j in two:
                        dve.wait_ge(y_added, CT * STEPS - CT + j + 1)
                        dve.bn_stats(stats[:, j, :], Y[:, NT - CT + j, :]).then_inc(stats_done, 1)
                    for j in two:
                        dve.wait_ge(stats_done, NT + j + 1)
                        dve.bn_aggr(mv3[:, j, :], stats[:, j, :]).then_inc(aggr_done, 1)
                    dve.wait_ge(aggr_done, NT + 2 * pr + 2)
                    c = slice(2 * pr, 2 * pr + 2)
                    dve.tensor_scalar(veps3[:, c], mv3[:, c, 1], EPS, None, ALU.add).then_inc(veps_done, 1)
                for j in range(CT):
                    dve.wait_ge(rstd_done, C + 1 + j // 2)
                    y = Y[:, NT - CT + j, :]
                    dve.tensor_scalar(y, y, mv3[:, j, 0:1], rstd3[:, j:j + 1], ALU.subtract, ALU.mult).then_inc(normed, 1)

            def statistics(c, done):
                for j in range(CT):
                    dve.bn_stats(stats[:, j, :], Y[:, CT * c + j, :]).then_inc(stats_done, 1)
                for j in range(CT):
                    dve.wait_ge(stats_done, CT * done + j + 1)
                    dve.bn_aggr(mv[:, j, :], stats[:, j, :]).then_inc(aggr_done, 1)
                dve.wait_ge(aggr_done, CT * done + CT)
                dve.tensor_scalar(veps[:], mv[:, :, 1], EPS, None, ALU.add).then_inc(veps_done, 1)

            def normalise(c, done):
                statistics(c, done)
                dve.wait_ge(rstd_done, done + 1)
                for j in range(CT):
                    y = Y[:, CT * c + j, :]
                    dve.tensor_scalar(y, y, mv[:, j, 0:1], rstd[:, j:j + 1], ALU.subtract, ALU.mult).then_inc(normed, 1)

            def turned(c):
                for j in range(CT):
                    i = CT * c + j
                    dve.wait_ge(x_hi, i + 1)
                    xs = (slice(None), i // TT, slice(None), slice(i % TT * P, (i % TT + 1) * P))
                    dve.tensor_tensor(XT[1][xs], bank[:, x_bank(i), :].rearrange("p (k t) -> p k t", k=KT),
                                      XT[0][xs].bitcast(F32), ALU.subtract).then_inc(x_lo, 1)

            def hidden(s, c):
                h = hs[c % 2]
                for f in range(FT):
                    dve.wait_ge(h_hi, FT * s + f + 1)
                    dve.tensor_tensor(h[1][:, f, :], h32[:, f, :], h[0][:, f, :].bitcast(F32), ALU.subtract).then_inc(h_lo, 1)

            def accumulate(s, c):
                for t in range(CT):
                    dve.wait_ge(y_done, CT * s + t + 1)
                    y = Y[:, CT * c + t, :]
                    dve.tensor_tensor(y, bank[:, Y0 + t, :], y, ALU.add).then_inc(y_added, 1)

            turned(0)
            for c in range(C):
                if c + 1 < C:
                    turned(c + 1)
                if c == 1:
                    normalise(C - 1, 0)
                hidden(c, c)
                if c:
                    dve.wait_ge(b2_added, CT * c)
                    accumulate(c - 1, c - 1)
            dve.wait_ge(b2_added, NT)
            with dve.Fori(1, G - 1) as g:
                for c in range(C):
                    hidden(g * C + c, c)
                    accumulate(g * C + c - 1, (c - 1) % C)
            hidden((G - 1) * C, 0)
            accumulate((G - 1) * C - 1, C - 1)
            for c in range(1, C):
                hidden((G - 1) * C + c, c)
                accumulate((G - 1) * C + c - 1, c - 1)
                dve.wait_ge(y_added, CT * ((G - 1) * C + c))
                if c < C - 1:
                    normalise(c - 1, c)
                else:
                    statistics(c - 1, c)
                    dve.tensor_scalar(nmean[:], mv[:, :, 0], -1.0, None, ALU.mult).then_inc(mean_negated, 1)
            normalise_last()

        @block.gpsimd
        def _(pool):
            def split(pair_w, raw, size, hi, lo, g):
                pool.wait_ge(hi, g + 1)
                pool.tensor_tensor(pair_w[1][:].rearrange("p a b -> p (a b)"), raw[:, 0:size],
                                   pair_w[0][:].rearrange("p a b -> p (a b)").bitcast(F32), ALU.subtract).then_inc(lo, 1)

            def rescale(n):
                pool.wait_ge(veps_done, n + 1)
                pool.tensor_tensor(rstd[:], veps[:], mhalf[:], ALU.pow).then_inc(rstd_done, 1)

            def add_b2(n):
                for j in range(CT):
                    i = CT * n + j
                    pool.wait_ge(x_turned, i + 1)
                    pool.tensor_tensor(Y[:, i, :], Y[:, i, :], b2[:], ALU.add).then_inc(b2_added, 1)

            pool.memset(mhalf[:], -0.5).then_inc(mhalf_set, 1)
            pool.wait_ge(mhalf_set, 1)
            split(W1, raw1, W1N, w1_hi, w1_lo, 0)
            split(W2, raw2, W2N, w2_hi, w2_lo, 0)
            add_b2(0)
            rescale(0)
            add_b2(1)
            add_b2(2)
            add_b2(3)
            with pool.Fori(1, G) as g:
                split(W1, raw1, W1N, w1_hi, w1_lo, g)
                split(W2, raw2, W2N, w2_hi, w2_lo, g)
            for n in range(C - 1):
                rescale(1 + n)
            pool.wait_ge(rstd_done, C)
            pool.wait_ge(mean_negated, 1)
            pool.tensor_tensor(shift[:], nmean[:], rstd[:], ALU.mult).then_inc(shift_set, 1)
            for pr in range(CT // 2):
                pool.wait_ge(veps_done, C + 1 + pr)
                c = slice(2 * pr, 2 * pr + 2)
                pool.tensor_tensor(rstd3[:, c], veps3[:, c], mhalf[:, c], ALU.pow).then_inc(rstd_done, 1)


def two_layers(nc, ins, out):
    x2 = nc.dram_tensor("x2", [P, B, TT, D], F32, kind="Internal").ap()
    x2T_hi = nc.dram_tensor("x2T_hi", [P, B, KT, S], F32, kind="Internal").ap()
    x2T_lo = nc.dram_tensor("x2T_lo", [P, B, KT, S], F32, kind="Internal").ap()
    with ExitStack() as ctx:
        def sb(name, shape, dt=F32):
            return ctx.enter_context(nc.sbuf_tensor("kept_" + name, shape, dt))

        stage, mask, ident = sb("stage", [P, 6 * D], F32R), sb("mask", [P, S]), sb("ident", [P, P])
        cos1, sin1 = sb("cos1", [P, S]), sb("sin1", [P, S])
        early = sb("early", [P, 2, KT, S], F32R)
        rows = sb("rows", [P, KT * S + 3 * D])
        x2T_stored = ctx.enter_context(nc.semaphore("x2T_stored"))
        first, queries = 2 * KT * P, KT * D
        later = ((stage[:, 0:first].bitcast(F32), ins["w_attn1"][:, 0, 0:first]), (cos1[:], ins["cos1"]), (sin1[:], ins["sin1"]))
        last = ((early[:, 0].bitcast(F32), x2T_hi[:, 0]), (early[:, 1].bitcast(F32), x2T_lo[:, 0]),
                (rows[:, 0:queries], ins["w_attn1"][:, 0, first:first + queries]))
        layer0(nc, ins["xT"], ins["x"], ins["w_qkv0"], ins["w_o0"], ins["w_base"], ins["w_lr"], ins["w_lb"], ins["b_base"],
               ins["b_router"], ins["cos0"], ins["sin0"], ins["mask"], ins["ident"], ins["inv_k"], x2, x2T_hi, x2T_lo,
               stage, mask, ident, later, early, rows, last, x2T_stored)
        Y, raw1, b2 = sb("Y", [P, NT, D]), sb("raw1", [P, 2 * KT * P + 2]), sb("b2", [P, D])
        attention1(nc, x2.rearrange("p b t d -> p (b t) d"), x2T_hi, x2T_lo, ins["w_attn1"], ins["w_ffn1"], ins["b2"],
                   cos1, sin1, mask, ident, stage, early, rows, raw1, b2, Y, x2T_stored)
        ffn1(nc, ins["w_ffn1"], ident, raw1, b2, out.rearrange("b (t p) d -> p (b t) d", p=P), Y)


def kernel(**inputs):
    import concourse.bacc as bacc
    from concourse.bass_utils import run_bass_kernel_spmd

    a = {name: np.asarray(v) for name, v in inputs.items()}

    def by_contraction(w):
        return w.reshape(KT, P, -1).transpose(1, 0, 2)

    def by_group(w):
        return w.reshape(KT, P, 8, -1).transpose(1, 2, 0, 3).reshape(P, 8, -1)

    def by_token_tile(t):
        return t.reshape(TT, P, -1).transpose(1, 0, 2)

    even_odd = np.concatenate([np.arange(0, 16, 2), np.arange(1, 16, 2)])

    def split_pairs(w):
        return w.reshape(D, -1, 16)[:, :, even_odd].reshape(D, -1)

    pos = np.arange(S, dtype=np.float32)[:, None]
    freq0 = 1.0 / np.float32(10000.0) ** (np.arange(0, 16, 2, dtype=np.float32) / np.float32(16))
    angle0 = pos * freq0.astype(np.float32)
    inv = 1.0 / 500000.0 ** (np.arange(0, 128, 2, dtype=np.float64) / 128)
    wavelen = 2.0 * np.pi / inv
    smooth = (1024 / wavelen - 1.0) / (4.0 - 1.0)
    scaled = np.where(wavelen > 1024 / 1.0, inv / 8.0, inv)
    mid = (wavelen <= 1024 / 1.0) & (wavelen >= 1024 / 4.0)
    scaled = np.where(mid, (1 - smooth) * inv / 8.0 + smooth * inv, scaled).astype(np.float32)
    angle1 = np.concatenate([pos * scaled[None, :]] * 2, axis=-1)
    sin1 = np.sin(angle1).T.copy()
    sin1[:P // 2] *= -1
    mask = np.zeros((P, S), np.float32)
    mask[:, P:] = np.where(np.arange(P)[:, None] >= np.arange(P)[None], 0, -1e30)

    x, wb = a["L0_attn_x"], a["L0_ffn_W_base"]
    lora_a = a["L0_ffn_lora_A"].transpose(1, 0, 2).reshape(D, -1)
    arrays = {
        "xT": x.reshape(B, S, KT, P).transpose(3, 0, 2, 1),
        "x": x.reshape(B, TT, P, D).transpose(2, 0, 1, 3),
        "w_qkv0": by_contraction(np.concatenate([split_pairs(a["L0_attn_Wq"]), split_pairs(a["L0_attn_Wk"]), a["L0_attn_Wv"]], 1)),
        "w_o0": by_contraction(a["L0_attn_Wo"]),
        "w_base": by_contraction(wb.T),
        "w_lr": by_contraction(np.concatenate([lora_a, a["L0_ffn_W_router"].T], 1)),
        "w_lb": a["L0_ffn_lora_B"].reshape(P, D),
        "b_base": a["L0_ffn_b_base"],
        "b_router": a["L0_ffn_b_router"],
        "cos0": by_token_tile(np.cos(np.concatenate([angle0, angle0], 1))),
        "sin0": by_token_tile(np.concatenate([-np.sin(angle0), np.sin(angle0)], 1)),
        "cos1": np.cos(angle1).T,
        "sin1": sin1,
        "mask": mask,
        "ident": np.eye(P),
        "inv_k": np.broadcast_to(1.0 / np.arange(1, 9), (P, 8)),
        "w_attn1": np.concatenate([by_group(a["L1_attn_wk"]), by_group(a["L1_attn_wv"]), by_group(a["L1_attn_wq"]),
                                   a["L1_attn_wo"].reshape(8, 4, P, D).transpose(2, 0, 1, 3).reshape(P, 8, -1)], 2),
        "w_ffn1": np.concatenate([by_group(a["L1_ffn_W1"]), a["L1_ffn_fc1_bias"].reshape(8, 2, P).transpose(2, 0, 1),
                                  a["L1_ffn_W2"].reshape(8, 2, P, D).transpose(2, 0, 1, 3).reshape(P, 8, -1)], 2),
        "b2": a["L1_ffn_fc2_bias"],
    }
    arrays = {name: np.ascontiguousarray(v, dtype=np.float32) for name, v in arrays.items()}
    nc = bacc.Bacc("TRN2", target_bir_lowering=False, num_devices=1)
    ins = {name: nc.dram_tensor(name, v.shape, F32, kind="ExternalInput").ap() for name, v in arrays.items()}
    out = nc.dram_tensor("out", (B, S, D), F32, kind="ExternalOutput").ap()
    two_layers(nc, ins, out)
    result = run_bass_kernel_spmd(nc, [arrays], core_ids=[0])
    return result.results[0]["out"]
```
